# Optimizing a Trainium2 kernel written in Bass

```python
import numpy as np
import jax
import jax.numpy as jnp

def _softmax(x, axis=-1):
    return jax.nn.softmax(x, axis=axis)

def _gelu(x):
    return jax.nn.gelu(x, approximate=True)

def _silu(x):
    return jax.nn.silu(x)

def _sigmoid(x):
    return jax.nn.sigmoid(x)

def _layernorm(x, axis=-1, eps=1e-05):
    m = jnp.mean(x, axis=axis, keepdims=True)
    v = jnp.var(x, axis=axis, keepdims=True)
    return (x - m) / jnp.sqrt(v + eps)

def _scatter_add(tgt, idx, src, axis=0):
    return tgt.at[idx].add(src)

def _segment_sum(src, seg, n):
    return jax.ops.segment_sum(src, seg, n)
kernel_name = 'mk_decoder_preln_d1_seqx_r8_efec87'

def setup_inputs(seed: int=0):
    np.random.seed(seed)
    _w = jnp.asarray

    def _rec_inputs():
        import jax
        import jax.numpy as jnp
        _rk = jax.random.key(seed)
        x = -0.0002928 + 1 * jax.random.normal(jax.random.fold_in(_rk, 1), (32, 128, 128), jnp.float32)
        _lenS = 128 - jax.random.randint(jax.random.fold_in(_rk, 7), (32,), 0, max(1, 128 // 4) + 1, jnp.int32)
        _lenS2 = 128 - jax.random.randint(jax.random.fold_in(_rk, 8), (32,), 0, max(1, 128 // 4) + 1, jnp.int32)
        _ctx_2048P = jax.random.normal(jax.random.fold_in(_rk, 11), (32, 16, 256), jnp.float32)
        _ctx_2048c = jax.random.dirichlet(jax.random.fold_in(_rk, 511), 0.3 * jnp.ones((16,), jnp.float32), (32, 128))
        _ctx_2048t = jnp.einsum('bsk,bkd->bsd', _ctx_2048c, _ctx_2048P)
        _ctx_2048t = _ctx_2048t * jax.lax.rsqrt(jnp.mean(jnp.square(_ctx_2048t)) + 1e-12) * 0.953939
        ctx_2048 = -0.000514642 + 1.00011 * (_ctx_2048t + 0.3 * jax.random.normal(jax.random.fold_in(_rk, 611), (32, 128, 256), jnp.float32))
        return (x, ctx_2048)
    x, ctx_2048 = _rec_inputs()

    def _L0_attn_setup():
        import jax, jax.numpy as jnp
        import numpy as np
        D_MODEL = 128
        N_HEADS = 16
        D_HEAD = 64
        VAR_EPS = 1e-05
        INIT_RANGE = 0.02
        B, S = (2, 256)

        def _layernorm(x, w, b):
            mean = jnp.mean(x, axis=-1, keepdims=True)
            var = jnp.var(x, axis=-1, keepdims=True)
            norm = (x - mean) / jnp.sqrt(var + VAR_EPS)
            return norm * w + b
        key = jax.random.key(seed)
        ks = jax.random.split(key, 6)
        resid_stream = jax.random.normal(ks[0], (B, S, D_MODEL), dtype=jnp.float32)
        attn_mask = jnp.ones((B, S), dtype=jnp.int32)
        W_q = jax.random.normal(ks[1], (N_HEADS, D_MODEL, D_HEAD), dtype=jnp.float32) * INIT_RANGE
        W_k = jax.random.normal(ks[2], (N_HEADS, D_MODEL, D_HEAD), dtype=jnp.float32) * INIT_RANGE
        W_v = jax.random.normal(ks[3], (N_HEADS, D_MODEL, D_HEAD), dtype=jnp.float32) * INIT_RANGE
        W_o = jax.random.normal(ks[4], (N_HEADS, D_HEAD, D_MODEL), dtype=jnp.float32) * INIT_RANGE
        b_q = jnp.zeros((N_HEADS, D_HEAD), dtype=jnp.float32)
        b_k = jnp.zeros((N_HEADS, D_HEAD), dtype=jnp.float32)
        b_v = jnp.zeros((N_HEADS, D_HEAD), dtype=jnp.float32)
        b_o = jnp.zeros((D_MODEL,), dtype=jnp.float32)
        ln_w = jnp.ones((D_MODEL,), dtype=jnp.float32)
        ln_b = jnp.zeros((D_MODEL,), dtype=jnp.float32)
        return dict(resid_stream=resid_stream, attn_mask=attn_mask, W_q=W_q, W_k=W_k, W_v=W_v, W_o=W_o, b_q=b_q, b_k=b_k, b_v=b_v, b_o=b_o, ln_w=ln_w, ln_b=ln_b)
    _L0_attn_all = _L0_attn_setup()
    _L0_attn_in = {k: v for k, v in _L0_attn_all.items() if k in ('attn_mask', 'W_q', 'W_k', 'W_v', 'W_o', 'b_q', 'b_k', 'b_v', 'b_o', 'ln_w', 'ln_b')}
    del _L0_attn_all

    def _L0_xattn_setup():
        import jax, jax.numpy as jnp
        import numpy as np
        NUM_HEADS = 16
        key = jax.random.key(seed)
        ks = jax.random.split(key, 5)
        dim = 128
        B, N, N_c = (4, 128, 32)
        x = jax.random.normal(ks[0], (B, N, dim), dtype=jnp.float32)
        context = jax.random.normal(ks[1], (B, N_c, 2 * dim), dtype=jnp.float32)
        w_qkv = jax.random.normal(ks[2], (3 * dim, dim), dtype=jnp.float32) * 0.02
        w_proj = jax.random.normal(ks[3], (dim, dim), dtype=jnp.float32) * 0.02
        b_proj = jax.random.normal(ks[4], (dim,), dtype=jnp.float32) * 0.02
        return {'x': x, 'context': context, 'w_qkv': w_qkv, 'w_proj': w_proj, 'b_proj': b_proj}
    _L0_xattn_all = _L0_xattn_setup()
    _L0_xattn_in = {k: v for k, v in _L0_xattn_all.items() if k in ('w_qkv', 'w_proj', 'b_proj')}
    del _L0_xattn_all

    def _L0_ffn_setup():
        import jax, jax.numpy as jnp
        import numpy as np
        NUM_EXPERTS = 8
        TOP_K = 2
        CAPACITY_FACTOR = 1.25
        key = jax.random.key(seed)
        ks = jax.random.split(key, 5)
        B, S, D, H, E = (4, 256, 128, 256, NUM_EXPERTS)
        scale = 0.02
        return {'x': jax.random.normal(ks[0], (B, S, D), dtype=jnp.float32), 'gate_w': jax.random.normal(ks[1], (E, D), dtype=jnp.float32) * scale, 'gate_proj_w': jax.random.normal(ks[2], (E, H, D), dtype=jnp.float32) * scale, 'up_proj_w': jax.random.normal(ks[3], (E, H, D), dtype=jnp.float32) * scale, 'down_proj_w': jax.random.normal(ks[4], (E, D, H), dtype=jnp.float32) * scale}
    _L0_ffn_all = _L0_ffn_setup()
    _L0_ffn_in = {k: v for k, v in _L0_ffn_all.items() if k in ('gate_w', 'gate_proj_w', 'up_proj_w', 'down_proj_w')}
    del _L0_ffn_all
    return {'x': x, 'ctx_2048': ctx_2048, 'L0_attn_attn_mask': _L0_attn_in['attn_mask'], 'L0_attn_W_q': _L0_attn_in['W_q'], 'L0_attn_W_k': _L0_attn_in['W_k'], 'L0_attn_W_v': _L0_attn_in['W_v'], 'L0_attn_W_o': _L0_attn_in['W_o'], 'L0_attn_b_q': _L0_attn_in['b_q'], 'L0_attn_b_k': _L0_attn_in['b_k'], 'L0_attn_b_v': _L0_attn_in['b_v'], 'L0_attn_b_o': _L0_attn_in['b_o'], 'L0_attn_ln_w': _L0_attn_in['ln_w'], 'L0_attn_ln_b': _L0_attn_in['ln_b'], 'L0_xattn_w_qkv': _L0_xattn_in['w_qkv'], 'L0_xattn_w_proj': _L0_xattn_in['w_proj'], 'L0_xattn_b_proj': _L0_xattn_in['b_proj'], 'L0_ffn_gate_w': _L0_ffn_in['gate_w'], 'L0_ffn_gate_proj_w': _L0_ffn_in['gate_proj_w'], 'L0_ffn_up_proj_w': _L0_ffn_in['up_proj_w'], 'L0_ffn_down_proj_w': _L0_ffn_in['down_proj_w']}

def reference(x, ctx_2048, L0_attn_attn_mask, L0_attn_W_q, L0_attn_W_k, L0_attn_W_v, L0_attn_W_o, L0_attn_b_q, L0_attn_b_k, L0_attn_b_v, L0_attn_b_o, L0_attn_ln_w, L0_attn_ln_b, L0_xattn_w_qkv, L0_xattn_w_proj, L0_xattn_b_proj, L0_ffn_gate_w, L0_ffn_gate_proj_w, L0_ffn_up_proj_w, L0_ffn_down_proj_w):
    import jax
    import jax.numpy as jnp

    def _L0_attn_ref(resid_stream, attn_mask, W_q, W_k, W_v, W_o, b_q, b_k, b_v, b_o, ln_w, ln_b):
        import jax, jax.numpy as jnp
        import numpy as np
        D_MODEL = 128
        N_HEADS = 16
        D_HEAD = 64
        VAR_EPS = 1e-05
        INIT_RANGE = 0.02
        B, S = (2, 256)

        def _layernorm(x, w, b):
            mean = jnp.mean(x, axis=-1, keepdims=True)
            var = jnp.var(x, axis=-1, keepdims=True)
            norm = (x - mean) / jnp.sqrt(var + VAR_EPS)
            return norm * w + b
        x = _layernorm(resid_stream, ln_w, ln_b)
        q = jnp.einsum('bsd,hde->bshe', x, W_q) + b_q
        k = jnp.einsum('bsd,hde->bshe', x, W_k) + b_k
        v = jnp.einsum('bsd,hde->bshe', x, W_v) + b_v
        scale = D_HEAD ** (-0.5)
        scores = jnp.einsum('bqhe,bkhe->bhqk', q, k) * scale
        sq, sk = (scores.shape[-2], scores.shape[-1])
        causal = jnp.tril(jnp.ones((sq, sk), dtype=bool))
        scores = jnp.where(causal, scores, -jnp.inf)
        pattern = jax.nn.softmax(scores, axis=-1)
        z = jnp.einsum('bhqk,bkhe->bqhe', pattern, v)
        attn_out = jnp.einsum('bqhe,hed->bqd', z, W_o) + b_o
        return attn_out

    def _L0_xattn_ref(x, context, w_qkv, w_proj, b_proj):
        import jax, jax.numpy as jnp
        import numpy as np
        NUM_HEADS = 16
        B, N, C = x.shape
        H = NUM_HEADS
        D = C // H
        scale = D ** (-0.5)
        qkv = (x @ w_qkv.T).reshape(B, N, 3, H, D).transpose(2, 0, 3, 1, 4)
        q, k, v = (qkv[0], qkv[1], qkv[2])
        N_c = context.shape[1]
        kv = context.reshape(B, N_c, 2, H, D).transpose(2, 0, 3, 1, 4)
        extra_k, extra_v = (kv[0], kv[1])
        k = jnp.concatenate([extra_k, k], axis=2)
        v = jnp.concatenate([extra_v, v], axis=2)
        dtype = q.dtype
        attn = jnp.einsum('bhnd,bhmd->bhnm', q * scale, k).astype(jnp.float32)
        attn = jax.nn.softmax(attn, axis=-1).astype(dtype)
        out = jnp.einsum('bhnm,bhmd->bhnd', attn, v)
        out = out.transpose(0, 2, 1, 3).reshape(B, N, C)
        return out @ w_proj.T + b_proj

    def _L0_ffn_ref(x, gate_w, gate_proj_w, up_proj_w, down_proj_w):
        import jax, jax.numpy as jnp
        import numpy as np
        NUM_EXPERTS = 8
        TOP_K = 2
        CAPACITY_FACTOR = 1.25
        B, S, D = x.shape
        E, K = (NUM_EXPERTS, TOP_K)
        T = B * S
        xf = x.reshape(T, D)
        logits = xf @ gate_w.T
        probs = jax.nn.softmax(logits, axis=-1)
        top_p, top_i = jax.lax.top_k(probs, K)
        w = top_p / (jnp.sum(top_p, axis=-1, keepdims=True) + 1e-09)
        capacity = int(CAPACITY_FACTOR * T / E)
        oh = jax.nn.one_hot(top_i, E, dtype=jnp.int32)
        rank = jnp.cumsum(oh, axis=0) - 1
        my_rank = jnp.sum(rank * oh, axis=-1)
        keep = (my_rank < capacity).astype(w.dtype)
        comb = jnp.einsum('tk,tke->te', w * keep, oh.astype(w.dtype))
        out = jnp.zeros_like(xf)
        for e in range(E):
            g = jax.nn.silu(xf @ gate_proj_w[e].T)
            u = xf @ up_proj_w[e].T
            y = g * u @ down_proj_w[e].T
            out = out + comb[:, e:e + 1] * y
        return out.reshape(B, S, D)
    x = x + _L0_attn_ref(_layernorm(x, axis=-1), L0_attn_attn_mask, L0_attn_W_q, L0_attn_W_k, L0_attn_W_v, L0_attn_W_o, L0_attn_b_q, L0_attn_b_k, L0_attn_b_v, L0_attn_b_o, L0_attn_ln_w, L0_attn_ln_b)
    x = x + _L0_xattn_ref(_layernorm(x, axis=-1), ctx_2048, L0_xattn_w_qkv, L0_xattn_w_proj, L0_xattn_b_proj)
    x = x + _L0_ffn_ref(_layernorm(x, axis=-1), L0_ffn_gate_w, L0_ffn_gate_proj_w, L0_ffn_up_proj_w, L0_ffn_down_proj_w)
    return x

_drawn_inputs = setup_inputs


def setup_inputs(seed=0):
    import zlib

    import numpy as np

    out = dict(_drawn_inputs(seed))
    spreads = {'L0_attn_b_q': (0.0, 0.8),
     'L0_attn_b_k': (0.0, 0.8),
     'L0_attn_b_v': (0.0, 0.1),
     'L0_attn_b_o': (0.0, 0.1),
     'L0_attn_ln_w': (1.0, 0.6),
     'L0_attn_ln_b': (0.0, 0.547)}
    factors = {'L0_attn_W_q': 8.0,
     'L0_attn_W_k': 8.0,
     'L0_xattn_w_qkv': 8.0,
     'L0_xattn_b_proj': 2.797,
     'L0_ffn_gate_w': 8.0,
     'L0_ffn_gate_proj_w': 8.0,
     'L0_ffn_up_proj_w': 8.0,
     'L0_ffn_down_proj_w': 8.0}
    for name, (base, spread) in spreads.items():
        noise = np.random.default_rng([zlib.crc32(name.encode()), seed]).standard_normal(out[name].shape)
        drawn = base * np.exp(spread * noise) if base else spread * noise
        out[name] = jnp.asarray(drawn.astype(out[name].dtype))
    for name, factor in factors.items():
        out[name] = (out[name] * factor).astype(out[name].dtype)
    return out
```

```python
from contextlib import ExitStack

import concourse.bass as bass
from concourse import mybir

F32 = mybir.dt.float32
BF16 = mybir.dt.bfloat16
F16 = mybir.dt.float16
U32 = mybir.dt.uint32
I32 = mybir.dt.int32
ALU = mybir.AluOpType
ACT = mybir.ActivationFunctionType
AX_X = mybir.AxisListType.X

P = 128
NB = 32
D = 128
H = 16
E1 = 64
PAIRS = H // 2
G1 = 4
HPG = H // G1
E2 = D // H
G2 = 8
KEYS2 = 2 * P
NE = 8
HID = 256
HT = HID // P
TOPK = 2
TOKENS = NB * P
CAPACITY = int(1.25 * TOKENS / NE)
CB = 4
NC = NB // CB
EPS = 1e-5
NORM_SCALE = 256.0
W_SCALE = 256.0
H_SCALE = 16.0
MASKED = -3.0e38
VGAP = 32
VPAD = VGAP - E2


def head2(n):
    return 4 * (n % 4) + n // 4


def run_batches(eng, lead, tail, body):
    def peeled(b):
        body(b, b % 2, lambda k: 0 <= b + k < NB)

    for b in range(-lead, 3):
        peeled(b)
    with eng.Fori(3, NB - 3, 2) as i:
        body(i, 1, lambda k: True)
        body(i + 1, 0, lambda k: True)
    for b in range(NB - 3, NB + tail):
        peeled(b)


def back(b, parity, g, k, n):
    off, unit = divmod(g - k, n)
    return off, unit, (parity + off) % 2


def build(nc, x, ctx, W_q, W_k, W_v, W_o, b_q, b_k, b_v, b_o, ln_w, ln_b, w_qkv, w_proj, b_proj,
          gate_w, gate_proj_w, up_proj_w, down_proj_w, out):
    es = ExitStack()
    with es:
        def sb(name, shape, dt=F32):
            return es.enter_context(nc.sbuf_tensor(name, shape, dt))

        def sem(name):
            return es.enter_context(nc.semaphore(name))

        es.enter_context(nc.allow_non_contiguous_dma(reason="small weights and biases, loaded once"))

        x_all = sb("x_all", [P, NB, D])
        ctx_row = sb("ctx_row", [P, 2, 2 * D])
        xnT_hi = sb("xnT_hi", [P, NB, P], F16)
        xnT_lo = sb("xnT_lo", [P, NB, P], F16)
        ident = sb("ident", [P, P])
        ident_b = sb("ident_b", [P, P], BF16)
        causal = sb("causal", [P, HPG, P], BF16)
        neg_half = sb("neg_half", [P, 1])
        jmask = sb("jmask", [P, 4])
        hmask = sb("hmask", [P, 4, 4])
        low_q = sb("low_q", [P, 1])
        low_k = sb("low_k", [P, 1])

        wq = sb("wq", [P, H, E1])
        wk = sb("wk", [P, H, E1])
        wv = sb("wv", [P, H, E1])
        wo = sb("wo", [P, PAIRS, D])
        bq = sb("bq", [P, PAIRS])
        bk = sb("bk", [P, PAIRS])
        bv = sb("bv", [P, PAIRS])
        bo = sb("bo", [P, D])
        bp = sb("bp", [P, D])
        lnw = sb("lnw", [P, 1])
        lnb = sb("lnb", [P, 1])

        wqkvT = sb("wqkvT", [P, 3, P])
        wprojT = sb("wprojT", [P, P])
        gateT = sb("gateT", [P, NE])
        w_hi = [sb(f"w_hi{i}", [P, NE * HT, P], F16) for i in range(3)]
        w_lo = [sb(f"w_lo{i}", [P, NE * HT, P], F16) for i in range(3)]
        upto = sb("upto", [P, P], BF16)
        ones_b = sb("ones_b", [P, P], BF16)
        rev_i = sb("rev_i", [P, NE], I32)
        rev = sb("rev", [P, NE])
        raw_s = sb("raw_s", [P, 5, P])

        qz = sb("qz", [P, 2, PAIRS, 2, P])
        kT = sb("kT", [P, 2, PAIRS, P])
        v1 = sb("v1", [P, 2, H * E1])
        probs = sb("probs", [P, 4, 512])
        probsT = sb("probsT", [P, 2, 512])
        zT = sb("zT", [P, PAIRS, P])
        nmax = sb("nmax", [P, 8, 4])
        rsum = sb("rsum", [P, 8, 4])
        rinv = sb("rinv", [P, 8, 4])
        bst = sb("bst", [P, 4, 6])
        mv = sb("mv", [P, 4, 2])
        ve = sb("ve", [P, 4])
        rstd = sb("rstd", [P, 4])
        zln = sb("zln", [P, D])
        xn = sb("xn", [P, D])
        xT = sb("xT", [P, P])

        wqR = sb("wqR", [P, 4, 4, 32])
        wkR = sb("wkR", [P, 4, 4, 32])
        keys4 = sb("keys4", [P, 4, 4, 32])
        q_hi = sb("q_hi", [P, 4, P], F16)
        k_hi = sb("k_hi", [P, 2, 4, P], F16)
        q_part = sb("q_part", [P, 4, P], F16)
        qm = sb("qm", [P, 2, H, P], F16)
        kT2 = sb("kT2", [P, 2, 4, KEYS2], F16)
        vm = sb("vm", [P, 2, 2, VPAD + H * VGAP])
        zT2 = sb("zT2", [P, P])
        xn2 = sb("xn2", [P, D])
        xT2 = sb("xT2", [P, P])
        xn3 = sb("xn3", [P, D])
        xT3 = sb("xT3", [P, P])
        logits = sb("logits", [P, NB, NE])
        gates = sb("gates", [P, NB, NE])
        rt_e = sb("rt_e", [P, NB, NE])
        rt_a = sb("rt_a", [P, NB])
        rt_b = sb("rt_b", [P, NB])
        topw = sb("topw", [P, NB, TOPK])
        chosen = sb("chosen", [P, NB, TOPK, NE])
        chosen_b = sb("chosen_b", [P, NB * TOPK * NE], BF16)
        scan = sb("scan", [P, 2, NB * TOPK * NE])
        comb = sb("comb", [P, NB, NE])
        silu = sb("silu", [P, HT, CB * P])
        hT = sb("hT", [P, HT, CB * P])
        h_hi = sb("h_hi", [P, 2, HT, CB * P], F16)
        h_lo = sb("h_lo", [P, 2, HT, CB * P], F16)
        raw_gu = qz[:, :, :, :, :].rearrange("p a t c q -> p (a t c) q")
        raw_d = kT[:, :, :, :].rearrange("p a t q -> p (a t) q")

        ps = [es.enter_context(nc.psum_tensor(f"ps{i}", [P, 512], F32)) for i in range(8)]

        alone = sem("alone")
        c_mem = sem("c_mem"); c_sel = sem("c_sel"); zeroed = sem("zeroed")
        ld_x0 = sem("ld_x0"); ld_x1 = sem("ld_x1"); ld_w1 = sem("ld_w1"); ld_wo = sem("ld_wo")
        ld_s = sem("ld_s"); ld_ctx = sem("ld_ctx"); ld_b = sem("ld_b"); wq_scaled = sem("wq_scaled"); bv_spread = sem("bv_spread"); bvo = sem("bvo")
        bo_ready = sem("bo_ready"); rep_ready = sem("rep_ready")
        ld_raw = sem("ld_raw"); raw_T = sem("raw_T"); raw_ev = sem("raw_ev"); w_staged = sem("w_staged"); w_ev = sem("w_ev");
        a_bn = sem("a_bn"); a_mv = sem("a_mv"); a_ve = sem("a_ve"); a_rstd = sem("a_rstd")
        a_z = sem("a_z"); a_bo = sem("a_bo"); a_xn = sem("a_xn")
        a_xT = sem("a_xT"); a_xTe = sem("a_xTe"); a_fill = sem("a_fill"); a_evq = sem("a_evq"); a_evv = sem("a_evv")
        a_s = sem("a_s"); a_max = sem("a_max"); a_exp = sem("a_exp"); a_rinv = sem("a_rinv")
        a_norm = sem("a_norm"); a_pT = sem("a_pT"); a_pTe = sem("a_pTe")
        a_zz = sem("a_zz"); a_ze = sem("a_ze"); a_o = sem("a_o"); a_res = sem("a_res")
        b_bn = sem("b_bn"); b_mv = sem("b_mv"); b_ve = sem("b_ve"); b_rstd = sem("b_rstd")
        b_bp = sem("b_bp"); b_xn = sem("b_xn"); b_vc = sem("b_vc")
        b_xT = sem("b_xT"); b_xTe = sem("b_xTe"); b_fill = sem("b_fill"); b_hi = sem("b_hi"); b_pack = sem("b_pack")
        b_vv = sem("b_vv"); b_keys4 = sem("b_keys4"); b_evac = sem("b_evac")
        b_s = sem("b_s"); b_max = sem("b_max"); b_exp = sem("b_exp"); b_rinv = sem("b_rinv")
        b_norm = sem("b_norm"); b_pT = sem("b_pT"); b_pTe = sem("b_pTe")
        b_zz = sem("b_zz"); b_ze = sem("b_ze"); b_pr = sem("b_pr"); b_res = sem("b_res")
        d_bn = sem("d_bn"); d_mv = sem("d_mv"); d_ve = sem("d_ve"); d_rstd = sem("d_rstd")
        d_xn = sem("d_xn"); d_xT = sem("d_xT"); d_xTe = sem("d_xTe"); d_hi = sem("d_hi"); d_cp = sem("d_cp")
        d_lg = sem("d_lg"); d_lge = sem("d_lge")
        r_shift = sem("r_shift"); r_exp = sem("r_exp"); r_step = sem("r_step"); r_chosen = sem("r_chosen")
        r_count_ps = sem("r_count_ps")
        f_gu = sem("f_gu"); f_s = sem("f_s"); f_h = sem("f_h"); f_hi = sem("f_hi"); f_lo0 = sem("f_lo0"); f_lo1 = sem("f_lo1"); f_y = sem("f_y"); f_acc = sem("f_acc")
        stored = sem("stored")

        block = es.enter_context(nc.Block())

        out_r = out.rearrange("b t d -> t b d")

        def bcast(ap, n):
            return ap.unsqueeze(2).to_broadcast([ap.shape[0], ap.shape[1], n])

        @block.sync
        def _(sp):
            xr = x.rearrange("b t d -> t b d")
            sp.dma_start(x_all[:, 0:4, :], xr[:, 0:4, :]).then_inc(ld_x0, 16)
            for dst, src in ((wq, W_q), (wk, W_k), (wv, W_v)):
                sp.dma_start(dst[:, :, :], src.rearrange("h d e -> d h e")).then_inc(ld_w1, 16)
            sp.dma_start(x_all[:, 4:NB, :], xr[:, 4:NB, :]).then_inc(ld_x1, 16)
            for a in range(2):
                wo_r = W_o.rearrange("(t a) e d -> a e t d", a=2)
                sp.dma_start(wo[64 * a:64 * a + 64, :, :], wo_r[a]).then_inc(ld_wo, 16)
            sp.dma_start(raw_s[:, 0:3, :], w_qkv.rearrange("(c p) d -> p c d", p=P)).then_inc(ld_s, 16)
            sp.dma_start(raw_s[:, 3, :], w_proj).then_inc(ld_s, 16)
            sp.dma_start(raw_s[0:NE, 4, :], gate_w).then_inc(ld_s, 16)

            def context(b, parity, valid):
                if valid(1):
                    n, np_ = b + 1, (parity + 1) % 2
                    if valid(0):
                        sp.wait_ge(ld_ctx, 16 * n)
                    if valid(-1):
                        sp.wait_ge(b_keys4, n - 1)
                        sp.wait_ge(b_vc, n - 1)
                    sp.dma_start(ctx_row[:, np_, :], ctx[n, :, :]).then_inc(ld_ctx, 16)

            sp.wait_ge(a_zz, G1 * NB)
            sp.dma_start(raw_gu[:, 0:16, :], gate_proj_w.rearrange("e (c p) d -> p (e c) d", p=P)).then_inc(ld_raw, 16)
            sp.dma_start(raw_gu[:, 16:32, :], up_proj_w.rearrange("e (c p) d -> p (e c) d", p=P)).then_inc(ld_raw, 16)
            sp.dma_start(raw_d.rearrange("p (e c) h -> p e (c h)", c=HT),
                         down_proj_w.rearrange("e d h -> d e h")).then_inc(ld_raw, 16)
            run_batches(sp, 1, 0, context)

            for c in range(1):
                sp.wait_ge(f_acc, NE)
                sp.dma_start(out_r[:, 0:CB, :], x_all[:, 0:CB, :]).then_inc(stored, 16)
            with sp.Fori(1, NC) as c:
                sp.wait_ge(f_acc, NE * c + NE)
                sp.dma_start(out_r[:, bass.ds(CB * c, CB), :], x_all[:, bass.ds(CB * c, CB), :]).then_inc(stored, 16)
            sp.wait_ge(stored, 16 * NC)

        @block.gpsimd
        def _(pool):
            nc.gpsimd.memset(ident[:, :], 0.0).then_inc(c_mem, 1)
            nc.gpsimd.memset(causal[:, :, :], 0.0).then_inc(c_mem, 1)
            nc.gpsimd.memset(hmask[:, :, :], 1.0).then_inc(c_mem, 1)
            nc.gpsimd.memset(neg_half[:, :], -0.5).then_inc(c_mem, 1)
            nc.gpsimd.memset(upto[:, :], 1.0).then_inc(c_mem, 1)
            nc.gpsimd.memset(ones_b[:, :], 1.0).then_inc(c_mem, 1)
            pool.wait_ge(c_mem, 6)
            nc.gpsimd.affine_select(out=ident[:, :], in_=ident[:, :], compare_op=ALU.not_equal, fill=1.0,
                                    base=0, pattern=[[-1, P]], channel_multiplier=1).then_inc(c_sel, 1)
            nc.gpsimd.affine_select(out=causal[:, :, :], in_=causal[:, :, :], compare_op=ALU.is_ge,
                                    fill=MASKED, base=0, pattern=[[0, HPG], [-1, P]],
                                    channel_multiplier=1).then_inc(c_sel, 1)
            nc.gpsimd.affine_select(out=hmask[:, :, :], in_=hmask[:, :, :], compare_op=ALU.is_ge, fill=0.0, base=0,
                                    pattern=[[-32, 4], [-E2, 4]], channel_multiplier=1).then_inc(c_sel, 1)
            nc.gpsimd.iota(rev_i[:, :], pattern=[[-1, NE]], base=NE, channel_multiplier=0).then_inc(c_sel, 1)
            nc.gpsimd.affine_select(out=upto[:, :], in_=upto[:, :], compare_op=ALU.is_ge, fill=0.0, base=0,
                                    pattern=[[1, P]], channel_multiplier=-1).then_inc(c_sel, 1)
            pool.wait_ge(c_sel, 5)
            nc.gpsimd.tensor_copy(rev[:, :], rev_i[:, :]).then_inc(c_sel, 1)
            nc.gpsimd.affine_select(out=hmask[:, :, :], in_=hmask[:, :, :], compare_op=ALU.is_ge, fill=0.0, base=E2 - 1,
                                    pattern=[[32, 4], [E2, 4]], channel_multiplier=-1).then_inc(c_sel, 1)
            nc.gpsimd.tensor_copy(ident_b[:, :], ident[:, :]).then_inc(c_sel, 1)

            pool.wait_ge(bo_ready, 1)
            pool.wait_ge(zeroed, 5)

            def self_attention(b, parity, valid):
                for g in range(G1):
                    off, u, _ = back(b, parity, g, 1, G1)
                    if valid(off):
                        t = G1 * (b + off) + u
                        pool.wait_ge(a_rinv, t + 1)
                        pr = probs[:, u, :].rearrange("p (h k) -> p h k", h=HPG)
                        nc.gpsimd.tensor_tensor(pr, pr, bcast(rinv[:, u, :], P), ALU.mult).then_inc(a_norm, 1)
                    if valid(2):
                        n = b + 2
                        if g < 2:
                            pool.wait_ge(a_mv, 2 * n + g + 1)
                            pool.sem_inc(alone)
                            nc.gpsimd.tensor_scalar(ve[:, g:g + 1], mv[:, g, 1:2], EPS, None,
                                                    ALU.add).then_inc(a_ve, 1)
                            pool.wait_ge(a_ve, 2 * n + g + 1)
                            nc.gpsimd.tensor_tensor(rstd[:, g:g + 1], ve[:, g:g + 1], neg_half[:, :],
                                                    ALU.pow).then_inc(a_rstd, 1)
                        if g == 2:
                            pool.wait_ge(a_z, n + 1)
                            nc.gpsimd.tensor_tensor(x_all[:, n, :], x_all[:, n, :], bo[:, :],
                                                    ALU.add).then_inc(a_bo, 1)

            run_batches(pool, 2, 1, self_attention)

            def cross_attention(b, parity, valid):
                for g in range(G2):
                    off, u, _ = back(b, parity, g, 1, G2)
                    if valid(off):
                        t = G2 * (b + off) + u
                        pool.wait_ge(b_rinv, t + 1)
                        pr = probs[:, u % 4, :].rearrange("p (h k) -> p h k", h=2)
                        nc.gpsimd.tensor_tensor(pr, pr, bcast(rinv[:, u, 0:2], KEYS2),
                                                ALU.mult).then_inc(b_norm, 1)
                    if valid(1):
                        n = b + 1
                        np_ = (parity + 1) % 2
                        if g == 0:
                            pool.wait_ge(b_mv, n + 1)
                            pool.sem_inc(alone)
                            nc.gpsimd.tensor_scalar(ve[:, 2:3], mv[:, 2, 1:2], EPS, None,
                                                    ALU.add).then_inc(b_ve, 1)
                            pool.wait_ge(b_ve, n + 1)
                            nc.gpsimd.tensor_tensor(rstd[:, 2:3], ve[:, 2:3], neg_half[:, :],
                                                    ALU.pow).then_inc(b_rstd, 1)
                        if g == 3:
                            pool.wait_ge(b_xn, n + 1)
                            nc.gpsimd.tensor_tensor(x_all[:, n, :], x_all[:, n, :], bp[:, :],
                                                    ALU.add).then_inc(b_bp, 1)
                        if g == 4:
                            if valid(-1):
                                pool.wait_ge(b_zz, n - 1)
                            pool.wait_ge(ld_ctx, 16 * n + 16)
                            dst = vm[:, np_, 0, VPAD:].rearrange("p (h c) -> p h c", c=VGAP)[:, :, 0:E2]
                            src = ctx_row[:, np_, D:2 * D].rearrange("p (h e) -> p h e", e=E2)
                            pool.sem_inc(alone)
                            nc.gpsimd.tensor_copy(dst, src).then_inc(b_vc, 1)
                    if valid(-1) and g == 5:
                        n = b - 1
                        pool.wait_ge(d_mv, n + 1)
                        pool.sem_inc(alone)
                        nc.gpsimd.tensor_scalar(ve[:, 3:4], mv[:, 3, 1:2], EPS, NORM_SCALE ** -2,
                                                ALU.add, ALU.mult).then_inc(d_ve, 1)
                        pool.wait_ge(d_ve, n + 1)
                        nc.gpsimd.tensor_tensor(rstd[:, 3:4], ve[:, 3:4], neg_half[:, :],
                                                ALU.pow).then_inc(d_rstd, 1)
                    if valid(-2) and g == 1:
                        n = b - 2
                        pool.wait_ge(d_xTe, n + 1)
                        pool.sem_inc(alone)
                        nc.gpsimd.tensor_copy(xnT_hi[:, n, :], xT3[:, :]).then_inc(d_hi, 1)
                        pool.wait_ge(d_hi, n + 1)
                        nc.gpsimd.tensor_tensor(xnT_lo[:, n, :], xT3[:, :], xnT_hi[:, n, :],
                                                ALU.subtract).then_inc(d_cp, 1)

            run_batches(pool, 1, 2, cross_attention)

            for i in range(3 * NE * HT // 4):
                pool.wait_ge(w_staged, i + 1)
                own = slice(4 * (i % 4), 4 * (i % 4) + 4)
                nc.gpsimd.tensor_tensor(w_lo[i // 4][:, own, :], hT[:, i % 2, :].rearrange("p (t q) -> p t q", t=4),
                                        w_hi[i // 4][:, own, :], ALU.subtract).then_inc(w_ev, 1)

            def experts(c, first):
                for e in range(NE):
                    t = NE * c + e
                    pool.wait_ge(f_hi, HT * t + 1)
                    if not (first and e < 2):
                        pool.wait_ge(f_y, t - 1)
                    nc.gpsimd.tensor_tensor(h_lo[:, e % 2, 0, :], hT[:, 0, :], h_hi[:, e % 2, 0, :],
                                            ALU.subtract).then_inc(f_lo0, 1)

            experts(0, True)
            with pool.Fori(1, NC) as c:
                experts(c, False)

        @block.scalar
        def _(act):
            for dst, src in ((bq, b_q), (bk, b_k), (bv, b_v)):
                for a in range(2):
                    act.dma_start(dst[64 * a:64 * a + 64, :],
                                  src.rearrange("(t a) e -> a e t", a=2)[a]).then_inc(ld_b, 16)
            act.dma_start(bo[:, :], b_o.rearrange("(o n) -> o n", o=1).to_broadcast([P, D])).then_inc(ld_b, 16)
            act.dma_start(bp[:, :], b_proj.rearrange("(o n) -> o n", o=1).to_broadcast([P, D])).then_inc(ld_b, 16)
            act.dma_start(lnw[:, :], ln_w.rearrange("(p o) -> p o", o=1)).then_inc(ld_b, 16)
            act.dma_start(lnb[:, :], ln_b.rearrange("(p o) -> p o", o=1)).then_inc(ld_b, 16)
            def self_attention(b, parity, valid):
                for g in range(G1):
                    off, u, _ = back(b, parity, g, 3, G1)
                    if valid(off):
                        t = G1 * (b + off) + u
                        act.wait_ge(a_zz, t + 1)
                        if u == 0 and valid(off - 1):
                            act.wait_ge(a_o, b + off)
                        nc.scalar.copy(zT[:, 2 * u:2 * u + 2, :], ps[6][:, 0:2 * P]).then_inc(a_ze, 1)
                    off, u, _ = back(b, parity, g, 2, G1)
                    if valid(off):
                        t = G1 * (b + off) + u
                        act.wait_ge(a_pT, t + 1)
                        nc.scalar.copy(probsT[:, u % 2, :], ps[2 + u % 2][:, :]).then_inc(a_pTe, 1)
                    if valid(0):
                        t = G1 * b + g
                        act.wait_ge(a_max, t + 1)
                        for i in range(HPG):
                            last = nc.scalar.activation(probs[:, g, i * P:(i + 1) * P],
                                                        ps[g % 2][:, i * P:(i + 1) * P], ACT.Exp,
                                                        bias=nmax[:, g, i:i + 1],
                                                        accum_out=rsum[:, g, i:i + 1])
                        last.then_inc(a_exp, 1)
                    if g == 2 and valid(1):
                        n, np_ = b + 1, (parity + 1) % 2
                        for half in range(2):
                            act.wait_ge(a_fill, 6 * n + 5 + half)
                            nc.scalar.copy(v1[:, np_, 512 * half:512 * half + 512], ps[4 + half][:, :]).then_inc(a_evv, 1)

            run_batches(act, 1, 1, self_attention)

            def cross_attention(b, parity, valid):
                for g in range(G2):
                    off, u, _ = back(b, parity, g, 3, G2)
                    if valid(off):
                        t = G2 * (b + off) + u
                        act.wait_ge(b_pT, t + 1)
                        nc.scalar.copy(probsT[:, u % 2, :], ps[2 + u % 2][:, :]).then_inc(b_pTe, 1)
                    if valid(0):
                        t = G2 * b + g
                        act.wait_ge(b_max, t + 1)
                        for i in range(2):
                            last = nc.scalar.activation(probs[:, g % 4, i * KEYS2:(i + 1) * KEYS2],
                                                        ps[g % 2][:, i * KEYS2:(i + 1) * KEYS2], ACT.Exp,
                                                        bias=nmax[:, g, i:i + 1],
                                                        accum_out=rsum[:, g, i:i + 1])
                        last.then_inc(b_exp, 1)
                    if valid(1):
                        n = b + 1
                        if g == 3:
                            act.wait_ge(b_fill, 3 * n + 1)
                            if valid(0):
                                act.wait_ge(b_pack, 3 * n)
                            nc.scalar.copy(q_hi[:, :, :], ps[4][:, :]).then_inc(b_hi, 1)
                            act.wait_ge(b_fill, 3 * n + 2)
                            nc.scalar.copy(k_hi[:, 0, :, :], ps[5][:, :]).then_inc(b_hi, 1)
                        if g == 5:
                            act.wait_ge(b_fill, 3 * n + 3)
                            nc.scalar.copy(k_hi[:, 1, :, :], ps[4][:, :]).then_inc(b_hi, 1)

            run_batches(act, 1, 1, cross_attention)

            act.wait_ge(r_shift, 1)
            nc.scalar.activation(gates[:, :, :], gates[:, :, :], ACT.Exp).then_inc(r_exp, 1)
            for i in range(3 * NE * HT // 4):
                act.wait_ge(raw_T, i + 3)
                nc.scalar.activation(w_hi[i // 4][:, 4 * (i % 4):4 * (i % 4) + 4, :], ps[i % 4][:, :], ACT.Copy,
                                     scale=W_SCALE)
                if i >= 2:
                    act.wait_ge(w_ev, i - 1)
                nc.scalar.activation(hT[:, i % 2, :], ps[i % 4][:, :], ACT.Copy, scale=W_SCALE).then_inc(w_staged, 1)

            def experts(c, first):
                for e in range(NE):
                    for i in range(HT):
                        n = HT * NE * c + HT * e + i
                        act.wait_ge(f_gu, n + 1)
                        if not (first and e == 0):
                            act.wait_ge(f_h, n - 1)
                        nc.scalar.activation(silu[:, i, :], ps[i][:, :], ACT.Silu,
                                             scale=1.0 / (NORM_SCALE * W_SCALE)).then_inc(f_s, 1)
                    for i in range(HT):
                        n = HT * NE * c + HT * e + i
                        act.wait_ge(f_h, n + 1)
                        if not (first and e < 2):
                            act.wait_ge(f_y, NE * c + e - 1)
                        nc.scalar.copy(h_hi[:, e % 2, i, :], hT[:, i, :]).then_inc(f_hi, 1)

            experts(0, True)
            with act.Fori(1, NC) as c:
                experts(c, False)

        @block.vector
        def _(dve):
            nc.vector.memset(qz[:, :, :, :, :], 0.0).then_inc(zeroed, 1)
            nc.vector.memset(vm[:, :, :, :], 0.0).then_inc(zeroed, 1)
            nc.vector.memset(low_q[0:64, :], 0.0)
            nc.vector.memset(low_q[64:P, :], -1.0).then_inc(zeroed, 1)
            for a in range(4):
                last = nc.vector.memset(low_k[32 * a:32 * a + 32, :], -float(a % 2))
            last.then_inc(zeroed, 1)
            dve.wait_ge(c_sel, 8)
            nc.vector.reduce_sum(jmask[:, :], hmask[:, :, :].rearrange("p a j -> p j a"), AX_X).then_inc(zeroed, 1)
            dve.wait_ge(zeroed, 5)
            dve.wait_ge(ld_b, 16 * 10)
            dve.wait_ge(ld_w1, 16 * 3)
            nc.vector.tensor_scalar(wq[:, :, :], wq[:, :, :], E1 ** -0.5, None, ALU.mult).then_inc(wq_scaled, 1)
            nc.vector.tensor_scalar(bq[:, :], bq[:, :], E1 ** -0.5, None, ALU.mult).then_inc(wq_scaled, 1)
            dve.wait_ge(ld_x0, 16)
            nc.vector.tensor_copy(v1[:, 0, :].rearrange("p (t q) -> p t q", t=PAIRS), bcast(bv[:, :], P)).then_inc(bv_spread, 1)
            dve.wait_ge(raw_T, 1)
            nc.vector.tensor_copy(wqkvT[:, :, :], ps[0][:, 0:3 * P]).then_inc(raw_ev, 1)
            nc.vector.tensor_copy(wprojT[:, :], ps[0][:, 3 * P:4 * P]).then_inc(raw_ev, 1)
            dve.wait_ge(raw_T, 2)
            nc.vector.tensor_scalar(gateT[:, :], ps[1][:, 0:NE], 1.0 / NORM_SCALE, None, ALU.mult).then_inc(raw_ev, 1)
            dve.wait_ge(bvo, 1)
            nc.vector.tensor_tensor(bo[:, :], ps[2][:, 0:P], bo[:, :], ALU.add).then_inc(bo_ready, 1)
            dve.wait_ge(raw_ev, 3)
            for dst, i, f in ((wqR, 0, E2 ** -0.5), (wkR, 1, 1.0)):
                for q4 in range(4):
                    nc.vector.tensor_scalar(dst[:, q4, :, :], wqkvT[:, i, 32 * q4:32 * q4 + 32].unsqueeze(1)
                                            .to_broadcast([P, 4, 32]), f, None, ALU.mult).then_inc(rep_ready, 1)

            def self_attention(b, parity, valid):
                for g in range(G1):
                    if g == 3 and valid(2):
                        dve.wait_ge(a_xT, b + 3)
                        if valid(1):
                            dve.wait_ge(a_fill, 6 * b + 12)
                        nc.vector.tensor_scalar(xT[:, :], ps[7][:, 0:P], lnw[:, :], lnb[:, :],
                                                ALU.mult, ALU.add).then_inc(a_xTe, 1)
                    if valid(0):
                        t = G1 * b + g
                        dve.wait_ge(a_s, t + 1)
                        nc.vector.reduce_max(nmax[:, g, :], ps[g % 2][:, :].rearrange("p (h k) -> p h k", h=HPG),
                                             AX_X, negate=True).then_inc(a_max, 1)
                    off, u, _ = back(b, parity, g, 1, G1)
                    if valid(off):
                        t = G1 * (b + off) + u
                        dve.wait_ge(a_exp, t + 1)
                        nc.vector.reciprocal(rinv[:, u, :], rsum[:, u, :]).then_inc(a_rinv, 1)
                    if valid(1) and g < 2:
                        n, np_ = b + 1, (parity + 1) % 2
                        for half in range(2):
                            dve.wait_ge(a_fill, 6 * n + 2 * g + half + 1)
                            tiles = ps[4 + half][:, :].rearrange("p (t q) -> p t q", t=4)
                            own = slice(4 * half, 4 * half + 4)
                            if g == 0:
                                for a in range(2):
                                    r = slice(64 * a, 64 * a + 64)
                                    last = nc.vector.tensor_tensor(qz[r, np_, own, a, :], tiles[r],
                                                                   bcast(bq[r, own], P), ALU.add)
                            else:
                                last = nc.vector.tensor_tensor(kT[:, np_, own, :], tiles,
                                                               bcast(bk[:, own], P), ALU.add)
                            last.then_inc(a_evq, 1)
                    if valid(2):
                        n = b + 2
                        if g == 0:
                            src = x_all[:, n, :]
                        if g == 1:
                            dve.wait_ge(a_rstd, 2 * n + 1)
                            nc.vector.tensor_scalar(zln[:, :], x_all[:, n, :], mv[:, 0, 0:1], rstd[:, 0:1],
                                                    ALU.subtract, ALU.mult).then_inc(a_z, 1)
                            dve.wait_ge(a_z, n + 1)
                            src = zln[:, :]
                        if g < 2:
                            dve.sem_inc(alone)
                            nc.vector.bn_stats(bst[:, g, :], src).then_inc(a_bn, 1)
                            dve.wait_ge(a_bn, 2 * n + g + 1)
                            dve.sem_inc(alone)
                            nc.vector.bn_aggr(mv[:, g, :], bst[:, g, :]).then_inc(a_mv, 1)
                        if g == 2:
                            dve.wait_ge(a_rstd, 2 * n + 2)
                            nc.vector.tensor_scalar(xn[:, :], zln[:, :], mv[:, 1, 0:1], rstd[:, 1:2],
                                                    ALU.subtract, ALU.mult).then_inc(a_xn, 1)
                    if g == 3 and valid(-1):
                        n = b - 1
                        dve.wait_ge(a_o, n + 1)
                        dve.wait_ge(a_bo, n + 1)
                        nc.vector.tensor_tensor(x_all[:, n, :], ps[7][:, P:2 * P], x_all[:, n, :],
                                                ALU.add).then_inc(a_res, 1)

            dve.wait_ge(ld_x0, 16)
            dve.wait_ge(ld_x1, 16)
            run_batches(dve, 2, 1, self_attention)

            dve.wait_ge(a_res, NB)

            def pack(dst, hi, bank, low):
                return nc.vector.scalar_tensor_tensor(out=dst, in0=hi, scalar=low[:, :], in1=bank,
                                                      op0=ALU.mult, op1=ALU.add)

            def cross_attention(b, parity, valid):
                for g in range(G2):
                    if valid(0):
                        t = G2 * b + g
                        dve.wait_ge(b_s, t + 1)
                        nc.vector.reduce_max(nmax[:, g, 0:2], ps[g % 2][:, :].rearrange("p (h k) -> p h k", h=2),
                                             AX_X, negate=True).then_inc(b_max, 1)
                    off, u, _ = back(b, parity, g, 1, G2)
                    if valid(off):
                        t = G2 * (b + off) + u
                        dve.wait_ge(b_exp, t + 1)
                        nc.vector.reciprocal(rinv[:, u, 0:2], rsum[:, u, 0:2]).then_inc(b_rinv, 1)
                    if valid(1):
                        n, np_ = b + 1, (parity + 1) % 2
                        if g == 0:
                            dve.sem_inc(alone)
                            nc.vector.bn_stats(bst[:, 2, :], x_all[:, n, :]).then_inc(b_bn, 1)
                            dve.wait_ge(b_bn, n + 1)
                            dve.sem_inc(alone)
                            nc.vector.bn_aggr(mv[:, 2, :], bst[:, 2, :]).then_inc(b_mv, 1)
                        if g == 1:
                            dve.wait_ge(b_rstd, n + 1)
                            nc.vector.tensor_scalar(xn2[:, :], x_all[:, n, :], mv[:, 2, 0:1], rstd[:, 2:3],
                                                    ALU.subtract, ALU.mult).then_inc(b_xn, 1)
                        if g == 2:
                            dve.wait_ge(b_xT, n + 1)
                            nc.vector.tensor_copy(xT2[:, :], ps[7][:, 0:P]).then_inc(b_xTe, 1)
                            dve.wait_ge(ld_ctx, 16 * n + 16)
                            quad = ctx_row[:, np_, 0:D].rearrange("p (g c) -> p g c", g=4)
                            nc.vector.tensor_copy(keys4[:, :, :, :], quad.unsqueeze(2).to_broadcast([P, 4, 4, 32])).then_inc(b_keys4, 1)
                        quads = [ps[k][:, :].rearrange("p (g q) -> p g q", g=4) for k in (4, 5)]
                        if g == 4:
                            dve.wait_ge(b_hi, 3 * n + 1)
                            pack(q_part[:, :, :], q_hi[:, :, :], quads[0], low_q).then_inc(b_pack, 1)
                            dve.wait_ge(b_hi, 3 * n + 2)
                            pack(kT2[:, np_, :, 0:P], k_hi[:, 0, :, :], quads[1], low_k).then_inc(b_pack, 1)
                        if g == 5:
                            dve.wait_ge(b_pack, 3 * n + 1)
                            for j in range(4):
                                nc.vector.tensor_scalar(qm[:, np_, 4 * j:4 * j + 4, :], q_part[:, :, :],
                                                        jmask[:, j:j + 1], None, ALU.mult)
                        if g == 6:
                            dve.wait_ge(b_hi, 3 * n + 3)
                            pack(kT2[:, np_, :, P:KEYS2], k_hi[:, 1, :, :], quads[0], low_k).then_inc(b_pack, 1)
                            dve.wait_ge(b_vv, n + 1)
                            dst = vm[:, np_, 1, VPAD:].rearrange("p (h c) -> p h c", c=VGAP)[:, :, 0:E2]
                            nc.vector.tensor_copy(dst, ps[5][:, 0:P].rearrange("p (h e) -> p h e", e=E2)).then_inc(b_evac, 1)
                    if valid(-1):
                        n = b - 1
                        if g == 3:
                            dve.wait_ge(b_zz, n + 1)
                            nc.vector.tensor_copy(zT2[:, :], ps[6][:, 0:P]).then_inc(b_ze, 1)
                        if g == 4:
                            dve.wait_ge(b_pr, n + 1)
                            dve.wait_ge(b_bp, n + 1)
                            nc.vector.tensor_tensor(x_all[:, n, :], ps[7][:, P:2 * P], x_all[:, n, :],
                                                    ALU.add).then_inc(b_res, 1)
                        if g == 5:
                            dve.wait_ge(b_res, n + 1)
                            dve.sem_inc(alone)
                            nc.vector.bn_stats(bst[:, 3, :], x_all[:, n, :]).then_inc(d_bn, 1)
                            dve.wait_ge(d_bn, n + 1)
                            dve.sem_inc(alone)
                            nc.vector.bn_aggr(mv[:, 3, :], bst[:, 3, :]).then_inc(d_mv, 1)
                        if g == 6:
                            dve.wait_ge(d_rstd, n + 1)
                            nc.vector.tensor_scalar(xn3[:, :], x_all[:, n, :], mv[:, 3, 0:1], rstd[:, 3:4],
                                                    ALU.subtract, ALU.mult).then_inc(d_xn, 1)
                        if g == 7:
                            dve.wait_ge(d_xT, n + 1)
                            if valid(-2):
                                dve.wait_ge(d_cp, n)
                            nc.vector.tensor_copy(xT3[:, :], ps[7][:, 2 * P:3 * P]).then_inc(d_xTe, 1)
                    if g == 1 and valid(-2):
                        n = b - 2
                        dve.wait_ge(d_lg, n + 1)
                        nc.vector.tensor_copy(logits[:, n, :], ps[7][:, 3 * P:3 * P + NE]).then_inc(d_lge, 1)
            run_batches(dve, 1, 2, cross_attention)

            dve.wait_ge(d_lge, NB)
            r_count = [0]

            def then(ins):
                r_count[0] += 1
                ins.then_inc(r_step, 1)
                dve.wait_ge(r_step, r_count[0])

            def over_e(ap):
                return ap.unsqueeze(2).to_broadcast([P, NB, NE])

            rev_b = rev[:, :].unsqueeze(1).to_broadcast([P, NB, NE])
            then(nc.vector.reduce_max(rt_a[:, :], logits[:, :, :], AX_X))
            nc.vector.tensor_tensor(gates[:, :, :], logits[:, :, :], over_e(rt_a[:, :]),
                                    ALU.subtract).then_inc(r_shift, 1)
            dve.wait_ge(r_exp, 1)
            then(nc.vector.reduce_sum(rt_a[:, :], gates[:, :, :], AX_X))
            then(nc.vector.reciprocal(rt_b[:, :], rt_a[:, :]))
            then(nc.vector.tensor_tensor(gates[:, :, :], gates[:, :, :], over_e(rt_b[:, :]), ALU.mult))
            for k in range(TOPK):
                top = topw[:, :, k]
                then(nc.vector.reduce_max(top, gates[:, :, :], AX_X))
                then(nc.vector.tensor_tensor(rt_e[:, :, :], gates[:, :, :], over_e(top), ALU.is_equal))
                then(nc.vector.tensor_tensor(rt_e[:, :, :], rt_e[:, :, :], rev_b, ALU.mult))
                then(nc.vector.reduce_max(rt_a[:, :], rt_e[:, :, :], AX_X))
                then(nc.vector.tensor_tensor(chosen[:, :, k, :], rev_b, over_e(rt_a[:, :]), ALU.is_equal))
                if k == 0:
                    then(nc.vector.scalar_tensor_tensor(out=gates[:, :, :], in0=chosen[:, :, k, :], scalar=-4.0,
                                                        in1=gates[:, :, :], op0=ALU.mult, op1=ALU.add))
            nc.vector.tensor_copy(chosen_b[:, :], chosen[:, :, :, :].rearrange("p b k e -> p (b k e)")).then_inc(r_chosen, 1)
            then(nc.vector.tensor_tensor(rt_a[:, :], topw[:, :, 0], topw[:, :, 1], ALU.add))
            then(nc.vector.tensor_scalar(rt_a[:, :], rt_a[:, :], 1e-9, None, ALU.add))
            then(nc.vector.reciprocal(rt_b[:, :], rt_a[:, :]))
            then(nc.vector.tensor_tensor(topw[:, :, :], topw[:, :, :], bcast(rt_b[:, :], TOPK), ALU.mult))
            dve.wait_ge(r_count_ps, 2)
            then(nc.vector.tensor_copy(scan[:, 0, :], ps[7][:, :]))
            cur, s, kk = 0, 1, TOPK * NE
            while s < NB:
                nc.vector.tensor_copy(scan[:, 1 - cur, 0:s * kk], scan[:, cur, 0:s * kk])
                then(nc.vector.tensor_tensor(scan[:, 1 - cur, s * kk:], scan[:, cur, s * kk:],
                                             scan[:, cur, 0:(NB - s) * kk], ALU.add))
                cur, s = 1 - cur, 2 * s
            ranks = scan[:, cur, :]
            then(nc.vector.tensor_tensor(ranks, ranks, ps[7][:, :], ALU.subtract))
            then(nc.vector.tensor_tensor(ranks, ranks, ps[6][:, :], ALU.add))
            ch = chosen[:, :, :, :].rearrange("p b k e -> p (b k e)")
            then(nc.vector.tensor_scalar(ranks, ranks, float(CAPACITY), None, ALU.is_le))
            then(nc.vector.tensor_tensor(ranks, ranks, ch, ALU.mult))
            rk = ranks.rearrange("p (c e) -> p c e", e=NE)
            then(nc.vector.tensor_tensor(rk, rk, bcast(topw[:, :, :].rearrange("p b k -> p (b k)"), NE), ALU.mult))
            r4 = ranks.rearrange("p (b k e) -> p b k e", k=TOPK, e=NE)
            then(nc.vector.tensor_tensor(comb[:, :, :], r4[:, :, 0, :], r4[:, :, 1, :], ALU.add))
            then(nc.vector.tensor_scalar(comb[:, :, :], comb[:, :, :], 1.0 / (H_SCALE * W_SCALE), None, ALU.mult))

            def add_up(c, e, have_before):
                t = NE * c + e
                dve.wait_ge(f_y, t + 1)
                if have_before:
                    dve.wait_ge(f_acc, t)
                for r in range(CB):
                    n = CB * c + r
                    last = nc.vector.scalar_tensor_tensor(out=x_all[:, n, :], in0=ps[4 + e % 2][:, r * P:(r + 1) * P],
                                                          scalar=comb[:, n, e:e + 1], in1=x_all[:, n, :],
                                                          op0=ALU.mult, op1=ALU.add)
                last.then_inc(f_acc, 1)

            def experts(c, first):
                for e in range(NE):
                    t = NE * c + e
                    for i in range(HT):
                        dve.wait_ge(f_s, HT * t + i + 1)
                        if not (first and e == 0):
                            dve.wait_ge((f_lo0, f_lo1)[i], t)
                        nc.vector.scalar_tensor_tensor(out=hT[:, i, :], in0=ps[2 + i][:, :],
                                                       scalar=H_SCALE / (NORM_SCALE * W_SCALE), in1=silu[:, i, :],
                                                       op0=ALU.mult, op1=ALU.mult).then_inc(f_h, 1)
                    dve.wait_ge(f_hi, HT * t + HT)
                    nc.vector.tensor_tensor(h_lo[:, e % 2, 1, :], hT[:, 1, :], h_hi[:, e % 2, 1, :],
                                            ALU.subtract).then_inc(f_lo1, 1)
                    if e > 0:
                        add_up(c, e - 1, not (first and e == 1))
                    elif not first:
                        add_up(c - 1, NE - 1, True)

            experts(0, True)
            with dve.Fori(1, NC) as c:
                experts(c, False)
            add_up(NC - 1, NE - 1, True)

        @block.tensor
        def _(pe):
            def mm(o, l, r, start=True, stop=True, **kw):
                return nc.tensor.matmul(o, l, r, start=start, stop=stop, **kw)

            pe.wait_ge(c_sel, 8)
            pe.wait_ge(ld_s, 16 * 3)
            for i in range(4):
                last = nc.tensor.transpose(ps[0][:, i * P:(i + 1) * P], raw_s[:, i, :], ident[:, :])
            last.then_inc(raw_T, 1)
            nc.tensor.transpose(ps[1][:, 0:NE], raw_s[0:NE, 4, :], ident[0:NE, 0:NE]).then_inc(raw_T, 1)
            pe.wait_ge(bv_spread, 1)
            pe.wait_ge(ld_wo, 32)
            for i in range(PAIRS):
                last = mm(ps[2][:, 0:P], v1[:, 0, i * P:(i + 1) * P], wo[:, i, :], i == 0, i == PAIRS - 1)
            last.then_inc(bvo, 1)
            pe.wait_ge(bo_ready, 1)
            pe.wait_ge(raw_ev, 3)
            pe.wait_ge(wq_scaled, 2)
            pe.wait_ge(zeroed, 5)

            def self_attention(b, parity, valid):
                for g in range(G1):
                    if g == 3 and valid(2):
                        pe.wait_ge(a_xn, b + 3)
                        if valid(-2):
                            pe.wait_ge(a_res, b - 1)
                        nc.tensor.transpose(ps[7][:, 0:P], xn[:, :], ident[:, :]).then_inc(a_xT, 1)
                    if valid(0):
                        t = G1 * b + g
                        if g == 0:
                            pe.wait_ge(a_evq, 4 * b + 4)
                        if g >= 2 or valid(-1):
                            pe.wait_ge(a_exp, t - 1)
                        bank = ps[g % 2]
                        mm(bank[:, :], ident_b[:, :], causal[:, :, :].rearrange("p h k -> p (h k)"), True, False)
                        for i in range(HPG):
                            h = HPG * g + i
                            last = mm(bank[:, i * P:(i + 1) * P], qz[:, parity, h // 2, h % 2, :],
                                      kT[:, parity, h // 2, :], False, i == HPG - 1)
                        last.then_inc(a_s, 1)
                    off, u, par = back(b, parity, g, 3, G1)
                    if valid(off):
                        t = G1 * (b + off) + u
                        pe.wait_ge(a_pTe, t + 1)
                        if u == 0:
                            pe.wait_ge(a_evv, 2 * (b + off) + 2)
                        if u > 0 or valid(off - 1):
                            pe.wait_ge(a_ze, t)
                        for i in range(HPG):
                            h = HPG * u + i
                            a = h % 2
                            last = mm(ps[6][64 * a:64 * a + 64, (i // 2) * P:(i // 2 + 1) * P],
                                      v1[:, par, h * E1:(h + 1) * E1], probsT[:, u % 2, i * P:(i + 1) * P])
                        last.then_inc(a_zz, 1)
                    off, u, par = back(b, parity, g, 2, G1)
                    if valid(off):
                        t = G1 * (b + off) + u
                        pe.wait_ge(a_norm, t + 1)
                        if u >= 2 or valid(off - 1):
                            pe.wait_ge(a_pTe, t - 1)
                        for i in range(HPG):
                            last = nc.tensor.transpose(ps[2 + u % 2][:, i * P:(i + 1) * P],
                                                       probs[:, u, i * P:(i + 1) * P], ident[:, :])
                        last.then_inc(a_pT, 1)
                    if g == 3 and valid(-1):
                        n = b - 1
                        pe.wait_ge(a_ze, G1 * n + G1)
                        if valid(2):
                            pe.wait_ge(a_xTe, b + 3)
                        for i in range(PAIRS):
                            last = mm(ps[7][:, P:2 * P], zT[:, i, :], wo[:, i, :], i == 0, i == PAIRS - 1)
                        last.then_inc(a_o, 1)
                    if valid(1) and g < 3:
                        n = b + 1
                        if g == 0:
                            pe.wait_ge(a_xTe, n + 1)
                        for half in range(2):
                            if g == 0 and valid(0):
                                pe.wait_ge(a_evv, 2 * n + half - 1)
                            if g > 0:
                                pe.wait_ge(a_evq, 4 * n + 2 * g + half - 1)
                            if g < 2:
                                w = wq if g == 0 else wk
                                for i in range(4):
                                    pair = 4 * half + i
                                    last = mm(ps[4 + half][:, i * P:(i + 1) * P],
                                              w[:, 2 * pair:2 * pair + 2, :].rearrange("p h e -> p (h e)"), xT[:, :])
                            else:
                                last = mm(ps[4 + half][:, :], xT[:, :],
                                          wv[:, 8 * half:8 * half + 8, :].rearrange("p h e -> p (h e)"))
                            last.then_inc(a_fill, 1)

            run_batches(pe, 2, 1, self_attention)
            pe.wait_ge(a_res, NB)
            pe.wait_ge(a_ze, G1 * NB)
            pe.wait_ge(rep_ready, 8)

            def cross_attention(b, parity, valid):
                for g in range(G2):
                    if valid(0):
                        t = G2 * b + g
                        if g == 0:
                            pe.wait_ge(b_evac, b + 1)
                        if g >= 2 or valid(-1):
                            pe.wait_ge(b_exp, t - 1)
                        for i in range(2):
                            last = mm(ps[g % 2][:, i * KEYS2:(i + 1) * KEYS2], qm[:, parity, 2 * g + i, :],
                                      kT2[:, parity, head2(2 * g + i) // 4, :])
                        last.then_inc(b_s, 1)
                    off, u, par = back(b, parity, g, 4, G2)
                    if valid(off):
                        t = G2 * (b + off) + u
                        pe.wait_ge(b_pTe, t + 1)
                        if u == 0:
                            pe.wait_ge(b_vc, b + off + 1)
                            if valid(off - 1):
                                pe.wait_ge(b_ze, b + off)
                        for k in range(2):
                            for i in range(2):
                                h = head2(2 * u + i)
                                q4, j = h // 4, h % 4
                                at = VPAD + VGAP * h - E2 * j
                                last = mm(ps[6][32 * q4:32 * q4 + 32, 0:P], vm[:, par, k, at:at + 32],
                                          probsT[:, u % 2, (2 * i + k) * P:(2 * i + k + 1) * P],
                                          j == 0 and k == 0, j == 3 and k == 1)
                        if u == G2 - 1:
                            last.then_inc(b_zz, 1)
                    off, u, par = back(b, parity, g, 3, G2)
                    if valid(off):
                        t = G2 * (b + off) + u
                        pe.wait_ge(b_norm, t + 1)
                        if u >= 2 or valid(off - 1):
                            pe.wait_ge(b_pTe, t - 1)
                        for i in range(4):
                            last = nc.tensor.transpose(ps[2 + u % 2][:, i * P:(i + 1) * P],
                                                       probs[:, u % 4, i * P:(i + 1) * P], ident[:, :])
                        last.then_inc(b_pT, 1)
                    if g == 0 and valid(-2):
                        pe.wait_ge(d_xTe, b - 1)
                        mm(ps[7][:, 3 * P:3 * P + NE], xT3[:, :], gateT[:, :]).then_inc(d_lg, 1)
                    if valid(1):
                        n = b + 1
                        if g == 2:
                            pe.wait_ge(b_xn, n + 1)
                            if valid(-2):
                                pe.wait_ge(d_lge, b - 1)
                            nc.tensor.transpose(ps[7][:, 0:P], xn2[:, :], ident[:, :]).then_inc(b_xT, 1)
                        if g == 3:
                            pe.wait_ge(b_xTe, n + 1)
                            if valid(0):
                                pe.wait_ge(b_evac, n)
                            for q4 in range(4):
                                last = mm(ps[4][:, q4 * P:(q4 + 1) * P],
                                          wqR[:, q4, :, :].rearrange("p a c -> p (a c)"), xT2[:, :])
                            last.then_inc(b_fill, 1)
                            pe.wait_ge(b_keys4, n + 1)
                            for q4 in range(4):
                                last = nc.tensor.transpose(ps[5][:, q4 * P:(q4 + 1) * P],
                                                           keys4[:, q4, :, :].rearrange("p a c -> p (a c)"), ident[:, :])
                            last.then_inc(b_fill, 1)
                        if g == 5:
                            pe.wait_ge(b_pack, 3 * n + 2)
                            for q4 in range(4):
                                last = mm(ps[4][:, q4 * P:(q4 + 1) * P],
                                          wkR[:, q4, :, :].rearrange("p a c -> p (a c)"), xT2[:, :])
                            last.then_inc(b_fill, 1)
                            mm(ps[5][:, 0:P], xT2[:, :], wqkvT[:, 2, :]).then_inc(b_vv, 1)
                    if g == 4 and valid(-1):
                        n = b - 1
                        pe.wait_ge(b_ze, n + 1)
                        if valid(1):
                            pe.wait_ge(b_xTe, b + 2)
                        mm(ps[7][:, P:2 * P], zT2[:, :], wprojT[:, :]).then_inc(b_pr, 1)
                    if g == 7 and valid(-1):
                        n = b - 1
                        pe.wait_ge(d_xn, n + 1)
                        pe.wait_ge(b_res, n + 1)
                        nc.tensor.transpose(ps[7][:, 2 * P:3 * P], xn3[:, :], ident[:, :]).then_inc(d_xT, 1)

            run_batches(pe, 1, 2, cross_attention)

            pe.wait_ge(ld_raw, 48)
            pe.wait_ge(d_lge, NB)
            for i in range(3 * NE * HT // 4):
                if i >= 4:
                    pe.wait_ge(w_staged, i - 3)
                for k in range(4):
                    raw = raw_gu[:, 4 * i + k, :] if i < 8 else raw_d[:, 4 * (i - 8) + k, :]
                    last = nc.tensor.transpose(ps[i % 4][:, k * P:(k + 1) * P], raw, ident[:, :])
                last.then_inc(raw_T, 1)
            pe.wait_ge(w_ev, 3 * NE * HT // 4)

            pe.wait_ge(r_chosen, 1)
            pe.wait_ge(d_cp, NB)
            mm(ps[6][:, :], upto[:, :], chosen_b[:, :]).then_inc(r_count_ps, 1)
            mm(ps[7][:, :], ones_b[:, :], chosen_b[:, :]).then_inc(r_count_ps, 1)

            def down(c, e, wait_bank):
                t = NE * c + e
                pe.wait_ge(f_hi, HT * t + HT)
                pe.wait_ge(f_lo0, t + 1)
                pe.wait_ge(f_lo1, t + 1)
                if wait_bank:
                    pe.wait_ge(f_acc, t - 1)
                for r in range(CB):
                    for i in range(HT):
                        own = slice(r * P, (r + 1) * P)
                        w = HT * e + i
                        for k, (h, v) in enumerate(((h_hi, w_hi), (h_hi, w_lo), (h_lo, w_hi))):
                            last = mm(ps[4 + e % 2][:, own], h[:, e % 2, i, own], v[2][:, w, :],
                                      i == 0 and k == 0, i == HT - 1 and k == 2)
                last.then_inc(f_y, 1)

            def experts(c, first):
                own = slice(0, CB) if first else bass.ds(CB * c, CB)
                rows_hi = xnT_hi[:, own, :].rearrange("p b t -> p (b t)")
                rows_lo = xnT_lo[:, own, :].rearrange("p b t -> p (b t)")
                for e in range(NE):
                    for i in range(HT):
                        if not (first and e == 0):
                            pe.wait_ge(f_h, HT * NE * c + HT * e + i - 1)
                        w = HT * e + i
                        for j in range(2):
                            mm(ps[2 * j + i][:, :], w_hi[j][:, w, :], rows_hi, True, False)
                            mm(ps[2 * j + i][:, :], w_hi[j][:, w, :], rows_lo, False, False)
                            last = mm(ps[2 * j + i][:, :], w_lo[j][:, w, :], rows_hi, False, True)
                        last.then_inc(f_gu, 1)
                    if e > 0:
                        down(c, e - 1, not (first and e < 3))
                    elif not first:
                        down(c - 1, NE - 1, True)

            experts(0, True)
            with pe.Fori(1, NC) as c:
                experts(c, False)
            down(NC - 1, NE - 1, True)


_INS = ["x", "ctx_2048", "L0_attn_W_q", "L0_attn_W_k", "L0_attn_W_v", "L0_attn_W_o", "L0_attn_b_q", "L0_attn_b_k",
        "L0_attn_b_v", "L0_attn_b_o", "L0_attn_ln_w", "L0_attn_ln_b", "L0_xattn_w_qkv", "L0_xattn_w_proj",
        "L0_xattn_b_proj", "L0_ffn_gate_w", "L0_ffn_gate_proj_w", "L0_ffn_up_proj_w", "L0_ffn_down_proj_w"]


def kernel(**inputs):
    import numpy as np
    from concourse import bacc
    from concourse.bass_utils import run_bass_kernel_spmd

    nc = bacc.Bacc("TRN2", target_bir_lowering=False, num_devices=1)
    arrays, args = {}, []
    for name in _INS:
        a = np.ascontiguousarray(inputs[name])
        arrays[f"in_{name}"] = a
        args.append(nc.dram_tensor(f"in_{name}", a.shape, mybir.dt.from_np(a.dtype), kind="ExternalInput").ap())
    args.append(nc.dram_tensor("out_x", (NB, P, D), F32, kind="ExternalOutput").ap())
    build(nc, *args)
    return run_bass_kernel_spmd(nc, [arrays], core_ids=[0]).results[0]["out_x"]
```

```python
from contextlib import ExitStack

import concourse.bass as bass
from concourse import mybir

F32 = mybir.dt.float32
BF16 = mybir.dt.bfloat16
F16 = mybir.dt.float16
U32 = mybir.dt.uint32
I32 = mybir.dt.int32
ALU = mybir.AluOpType
ACT = mybir.ActivationFunctionType
AX_X = mybir.AxisListType.X

P = 128
NB = 32
D = 128
H = 16
E1 = 64
PAIRS = H // 2
G1 = 4
HPG = H // G1
E2 = D // H
G2 = 8
KEYS2 = 2 * P
NE = 8
HID = 256
HT = HID // P
TOPK = 2
TOKENS = NB * P
CAPACITY = int(1.25 * TOKENS / NE)
CB = 4
NC = NB // CB
EPS = 1e-5
X1_SCALE = 16.0
NORM_SCALE = 256.0
W_SCALE = 256.0
H_SCALE = 16.0
MASKED = -3.0e38
VGAP = 32
VPAD = VGAP - E2


def head2(n):
    return 4 * (n % 4) + n // 4


PT_ON_VECTOR = (6,)
SCORE_BANKS2 = (0, 1, 5, 0, 1, 5, 0, 1)


def run_batches(eng, lead, tail, body):
    def peeled(b):
        body(b, b % 2, lambda k: 0 <= b + k < NB)

    for b in range(-lead, 3):
        peeled(b)
    with eng.Fori(3, NB - 3, 2) as i:
        body(i, 1, lambda k: True)
        body(i + 1, 0, lambda k: True)
    for b in range(NB - 3, NB + tail):
        peeled(b)


def back(b, parity, g, k, n):
    off, unit = divmod(g - k, n)
    return off, unit, (parity + off) % 2


def build(nc, x, ctx, W_q, W_k, W_v, W_o, b_q, b_k, b_v, b_o, ln_w, ln_b, w_qkv, w_proj, b_proj,
          gate_w, gate_proj_w, up_proj_w, down_proj_w, out):
    es = ExitStack()
    with es:
        def sb(name, shape, dt=F32):
            return es.enter_context(nc.sbuf_tensor(name, shape, dt))

        def sem(name):
            return es.enter_context(nc.semaphore(name))

        es.enter_context(nc.allow_non_contiguous_dma(reason="small weights and biases, loaded once"))

        x_all = sb("x_all", [P, NB, D])
        ctx_row = sb("ctx_row", [P, 2, 2 * D])
        xnT_hi = sb("xnT_hi", [P, NB, P], F16)
        xnT_lo = sb("xnT_lo", [P, NB, P], F16)
        ident = sb("ident", [P, P])
        ident_b = sb("ident_b", [P, P], BF16)
        ident_h = sb("ident_h", [P, P], F16)
        causal = sb("causal", [P, HPG, P], BF16)
        neg_half = sb("neg_half", [P, 1])
        jmask = sb("jmask", [P, 4])
        hmask = sb("hmask", [P, 4, 4])
        low_q = sb("low_q", [P, 1])
        low_k = sb("low_k", [P, 1])

        wq = sb("wq", [P, H, E1])
        wk = sb("wk", [P, H, E1])
        wv = sb("wv", [P, H, E1])
        w1_hi = sb("w1_hi", [P, 3, H, E1], F16)
        w1_lo = sb("w1_lo", [P, 3, H, E1], F16)
        wo = sb("wo", [P, PAIRS, D])
        bq = sb("bq", [P, PAIRS])
        bk = sb("bk", [P, PAIRS])
        bv = sb("bv", [P, PAIRS])
        bo = sb("bo", [P, D])
        bp = sb("bp", [P, D])
        lnw = sb("lnw", [P, 1])
        lnb = sb("lnb", [P, 1])

        wqkvT = sb("wqkvT", [P, 3, P])
        wprojT = sb("wprojT", [P, P])
        gateT = sb("gateT", [P, NE])
        w_hi = [sb(f"w_hi{i}", [P, NE * HT, P], F16) for i in range(3)]
        w_lo = [sb(f"w_lo{i}", [P, NE * HT, P], F16) for i in range(3)]
        upto = sb("upto", [P, P], BF16)
        ones_b = sb("ones_b", [P, P], BF16)
        rev_i = sb("rev_i", [P, NE], I32)
        rev = sb("rev", [P, NE])
        raw_s = sb("raw_s", [P, 5, P])

        qz = sb("qz", [P, 2, PAIRS, 2, P])
        kT = sb("kT", [P, 2, PAIRS, P])
        v1 = sb("v1", [P, 2, H * E1])
        probs = sb("probs", [P, 4, 512])
        probsT = sb("probsT", [P, 4, 512])
        zT = sb("zT", [P, PAIRS, P])
        nmax = sb("nmax", [P, 8, 4])
        rsum = sb("rsum", [P, 8, 4])
        rinv = sb("rinv", [P, 8, 4])
        bst = sb("bst", [P, 4, 6])
        mv = sb("mv", [P, 4, 2])
        ve = sb("ve", [P, 4])
        rstd = sb("rstd", [P, 4])
        zln = sb("zln", [P, D])
        xn = sb("xn", [P, D])
        xT = sb("xT", [P, P])
        xT_hi = sb("xT_hi", [P, P], F16)
        xT_lo = sb("xT_lo", [P, P], F16)

        wqR = sb("wqR", [P, 4, 4, 32])
        wkR = sb("wkR", [P, 4, 4, 32])
        keys4 = sb("keys4", [P, 4, 2, 2, 32], F16)
        q_hi = sb("q_hi", [P, 4, P], F16)
        k_hi = sb("k_hi", [P, 4, P], F16)
        q_part = sb("q_part", [P, 4, P], F16)
        qm = sb("qm", [P, 2, H, P], F16)
        kT2 = sb("kT2", [P, 2, 4, KEYS2], F16)
        vm = sb("vm", [P, 2, 2, VPAD + H * VGAP])
        zT2 = sb("zT2", [P, P])
        rsum2 = sb("rsum2", [P, 2, H])
        rinv2 = sb("rinv2", [P, H])
        rinv_wide = sb("rinv_wide", [P, H, E2])
        rinvT = sb("rinvT", [P, P])
        xn2 = sb("xn2", [P, D])
        xT2 = sb("xT2", [P, P])
        xn3 = sb("xn3", [P, D])
        xT3 = sb("xT3", [P, P])
        logits = sb("logits", [P, NB, NE])
        gates = sb("gates", [P, NB, NE])
        rt_e = sb("rt_e", [P, NB, NE])
        rt_a = sb("rt_a", [P, NB])
        rt_b = sb("rt_b", [P, NB])
        topw = sb("topw", [P, NB, TOPK])
        chosen = sb("chosen", [P, NB, TOPK, NE])
        chosen_b = sb("chosen_b", [P, NB * TOPK * NE], BF16)
        scan = sb("scan", [P, 2, NB * TOPK * NE])
        comb = sb("comb", [P, NB, NE])
        silu = wq[:, :, :].rearrange("p (i h) e -> p i (h e)", i=HT)
        hT = wk[:, :, :].rearrange("p (i h) e -> p i (h e)", i=HT)
        h_hi = sb("h_hi", [P, 2, HT, CB * P], F16)
        h_lo = sb("h_lo", [P, 2, HT, CB * P], F16)
        raw_gu = qz[:, :, :, :, :].rearrange("p a t c q -> p (a t c) q")
        raw_d = kT[:, :, :, :].rearrange("p a t q -> p (a t) q")

        ps = [es.enter_context(nc.psum_tensor(f"ps{i}", [P, 512], F32)) for i in range(8)]

        alone = sem("alone")
        c_mem = sem("c_mem"); c_sel = sem("c_sel"); zeroed = sem("zeroed")
        ld_x0 = sem("ld_x0"); ld_x1 = sem("ld_x1"); ld_w = [sem(f"ld_w{i}") for i in range(3)]; ld_wo = sem("ld_wo")
        ld_s = sem("ld_s"); ld_ctx = sem("ld_ctx"); ld_b = sem("ld_b"); w1_hi_done = sem("w1_hi_done"); w1_split = sem("w1_split"); b1_scaled = sem("b1_scaled"); bv_spread = sem("bv_spread"); bvo = sem("bvo")
        bo_ready = sem("bo_ready"); rep_ready = sem("rep_ready")
        ld_raw = sem("ld_raw"); raw_T = sem("raw_T"); raw_ev = sem("raw_ev"); w_staged = sem("w_staged"); w_ev = sem("w_ev");
        a_bn = sem("a_bn"); a_mv = sem("a_mv"); a_ve = sem("a_ve"); a_rstd = sem("a_rstd")
        a_z = sem("a_z"); a_bo = sem("a_bo"); a_xn = sem("a_xn")
        a_xT = sem("a_xT"); a_xTe = sem("a_xTe"); a_xhi = sem("a_xhi"); a_xlo = sem("a_xlo"); a_fill = sem("a_fill"); a_evq = sem("a_evq"); a_evv = sem("a_evv")
        a_s = sem("a_s"); a_max = sem("a_max"); a_exp = sem("a_exp"); a_rinv = sem("a_rinv")
        a_norm = sem("a_norm"); a_pT = sem("a_pT"); a_pTe = sem("a_pTe")
        a_zz = sem("a_zz"); a_ze = sem("a_ze"); a_o = sem("a_o"); a_res = sem("a_res")
        b_bn = sem("b_bn"); b_mv = sem("b_mv"); b_ve = sem("b_ve"); b_rstd = sem("b_rstd")
        b_bp = sem("b_bp"); b_xn = sem("b_xn"); b_vc = sem("b_vc")
        b_xT = sem("b_xT"); b_xTe = sem("b_xTe"); b_fill = sem("b_fill"); b_hi = sem("b_hi"); b_pack = sem("b_pack")
        b_vv = sem("b_vv"); b_vve = sem("b_vve"); b_keys4 = sem("b_keys4"); b_evac = sem("b_evac")
        b_khi = sem("b_khi")
        b_s = sem("b_s"); b_max = sem("b_max"); b_exp = sem("b_exp"); b_rinv = sem("b_rinv")
        b_wide = sem("b_wide"); b_rT = sem("b_rT"); b_rTe = sem("b_rTe")
        b_pT = sem("b_pT"); b_pTa = sem("b_pTa"); b_pTv = sem("b_pTv")
        b_zz = sem("b_zz"); b_ze = sem("b_ze"); b_pr = sem("b_pr"); b_res = sem("b_res")
        d_bn = sem("d_bn"); d_mv = sem("d_mv"); d_ve = sem("d_ve"); d_rstd = sem("d_rstd")
        d_xn = sem("d_xn"); d_xT = sem("d_xT"); d_xTe = sem("d_xTe"); d_hi = sem("d_hi"); d_cp = sem("d_cp")
        d_lg = sem("d_lg"); d_lge = sem("d_lge")
        r_shift = sem("r_shift"); r_exp = sem("r_exp"); r_step = sem("r_step"); r_chosen = sem("r_chosen")
        r_count_ps = sem("r_count_ps")
        f_gu = sem("f_gu"); f_s = sem("f_s"); f_h = sem("f_h"); f_hi = sem("f_hi"); f_lo0 = sem("f_lo0"); f_lo1 = sem("f_lo1"); f_y = sem("f_y"); f_acc = sem("f_acc")
        stored = sem("stored")

        block = es.enter_context(nc.Block())

        out_r = out.rearrange("b t d -> t b d")

        def bcast(ap, n):
            return ap.unsqueeze(2).to_broadcast([ap.shape[0], ap.shape[1], n])

        @block.sync
        def _(sp):
            xr = x.rearrange("b t d -> t b d")
            sp.dma_start(x_all[:, 0:4, :], xr[:, 0:4, :]).then_inc(ld_x0, 16)
            for dst, src, loaded in ((wq, W_q, ld_w[0]), (wk, W_k, ld_w[1]), (wv, W_v, ld_w[2])):
                sp.dma_start(dst[:, :, :], src.rearrange("h d e -> d h e")).then_inc(loaded, 16)
            sp.dma_start(x_all[:, 4:NB, :], xr[:, 4:NB, :]).then_inc(ld_x1, 16)
            for a in range(2):
                wo_r = W_o.rearrange("(t a) e d -> a e t d", a=2)
                sp.dma_start(wo[64 * a:64 * a + 64, :, :], wo_r[a]).then_inc(ld_wo, 16)
            sp.dma_start(raw_s[:, 0:3, :], w_qkv.rearrange("(c p) d -> p c d", p=P)).then_inc(ld_s, 16)
            sp.dma_start(raw_s[:, 3, :], w_proj).then_inc(ld_s, 16)
            sp.dma_start(raw_s[0:NE, 4, :], gate_w).then_inc(ld_s, 16)

            def context(b, parity, valid):
                if valid(1):
                    n, np_ = b + 1, (parity + 1) % 2
                    if valid(0):
                        sp.wait_ge(ld_ctx, 16 * n)
                    if valid(-1):
                        sp.wait_ge(b_keys4, n - 1)
                        sp.wait_ge(b_vc, n - 1)
                    sp.dma_start(ctx_row[:, np_, :], ctx[n, :, :]).then_inc(ld_ctx, 16)

            sp.wait_ge(a_zz, G1 * NB)
            sp.dma_start(raw_gu[:, 0:16, :], gate_proj_w.rearrange("e (c p) d -> p (e c) d", p=P)).then_inc(ld_raw, 16)
            sp.dma_start(raw_gu[:, 16:32, :], up_proj_w.rearrange("e (c p) d -> p (e c) d", p=P)).then_inc(ld_raw, 16)
            sp.dma_start(raw_d.rearrange("p (e c) h -> p e (c h)", c=HT),
                         down_proj_w.rearrange("e d h -> d e h")).then_inc(ld_raw, 16)
            run_batches(sp, 1, 0, context)

            for c in range(1):
                sp.wait_ge(f_acc, NE)
                sp.dma_start(out_r[:, 0:CB, :], x_all[:, 0:CB, :]).then_inc(stored, 16)
            with sp.Fori(1, NC) as c:
                sp.wait_ge(f_acc, NE * c + NE)
                sp.dma_start(out_r[:, bass.ds(CB * c, CB), :], x_all[:, bass.ds(CB * c, CB), :]).then_inc(stored, 16)
            sp.wait_ge(stored, 16 * NC)

        @block.gpsimd
        def _(pool):
            nc.gpsimd.memset(ident[:, :], 0.0).then_inc(c_mem, 1)
            nc.gpsimd.memset(causal[:, :, :], 0.0).then_inc(c_mem, 1)
            nc.gpsimd.memset(hmask[:, :, :], 1.0).then_inc(c_mem, 1)
            nc.gpsimd.memset(neg_half[:, :], -0.5).then_inc(c_mem, 1)
            nc.gpsimd.memset(upto[:, :], 1.0).then_inc(c_mem, 1)
            nc.gpsimd.memset(ones_b[:, :], 1.0).then_inc(c_mem, 1)
            pool.wait_ge(c_mem, 6)
            nc.gpsimd.affine_select(out=ident[:, :], in_=ident[:, :], compare_op=ALU.not_equal, fill=1.0,
                                    base=0, pattern=[[-1, P]], channel_multiplier=1).then_inc(c_sel, 1)
            nc.gpsimd.affine_select(out=causal[:, :, :], in_=causal[:, :, :], compare_op=ALU.is_ge,
                                    fill=MASKED, base=0, pattern=[[0, HPG], [-1, P]],
                                    channel_multiplier=1).then_inc(c_sel, 1)
            nc.gpsimd.affine_select(out=hmask[:, :, :], in_=hmask[:, :, :], compare_op=ALU.is_ge, fill=0.0, base=0,
                                    pattern=[[-32, 4], [-E2, 4]], channel_multiplier=1).then_inc(c_sel, 1)
            nc.gpsimd.iota(rev_i[:, :], pattern=[[-1, NE]], base=NE, channel_multiplier=0).then_inc(c_sel, 1)
            nc.gpsimd.affine_select(out=upto[:, :], in_=upto[:, :], compare_op=ALU.is_ge, fill=0.0, base=0,
                                    pattern=[[1, P]], channel_multiplier=-1).then_inc(c_sel, 1)
            pool.wait_ge(c_sel, 5)
            nc.gpsimd.tensor_copy(rev[:, :], rev_i[:, :]).then_inc(c_sel, 1)
            nc.gpsimd.affine_select(out=hmask[:, :, :], in_=hmask[:, :, :], compare_op=ALU.is_ge, fill=0.0, base=E2 - 1,
                                    pattern=[[32, 4], [E2, 4]], channel_multiplier=-1).then_inc(c_sel, 1)
            nc.gpsimd.tensor_copy(ident_b[:, :], ident[:, :]).then_inc(c_sel, 1)
            nc.gpsimd.tensor_copy(ident_h[:, :], ident[:, :]).then_inc(c_sel, 1)

            pool.wait_ge(bo_ready, 1)
            pool.wait_ge(zeroed, 5)

            def self_attention(b, parity, valid):
                for g in range(G1):
                    if g == 3 and valid(2):
                        n = b + 2
                        pool.wait_ge(a_xTe, n + 1)
                        if valid(1):
                            pool.wait_ge(a_fill, 6 * b + 12)
                        pool.sem_inc(alone)
                        nc.gpsimd.tensor_copy(xT_hi[:, :], xT[:, :]).then_inc(a_xhi, 1)
                        pool.wait_ge(a_xhi, n + 1)
                        nc.gpsimd.tensor_tensor(xT_lo[:, :], xT[:, :], xT_hi[:, :], ALU.subtract).then_inc(a_xlo, 1)
                    off, u, _ = back(b, parity, g, 1, G1)
                    if valid(off):
                        t = G1 * (b + off) + u
                        pool.wait_ge(a_rinv, t + 1)
                        pr = probs[:, u, :].rearrange("p (h k) -> p h k", h=HPG)
                        nc.gpsimd.tensor_tensor(pr, pr, bcast(rinv[:, u, :], P), ALU.mult).then_inc(a_norm, 1)
                    if valid(2):
                        n = b + 2
                        if g < 2:
                            pool.wait_ge(a_mv, 2 * n + g + 1)
                            pool.sem_inc(alone)
                            nc.gpsimd.tensor_scalar(ve[:, g:g + 1], mv[:, g, 1:2], EPS, None,
                                                    ALU.add).then_inc(a_ve, 1)
                            pool.wait_ge(a_ve, 2 * n + g + 1)
                            nc.gpsimd.tensor_tensor(rstd[:, g:g + 1], ve[:, g:g + 1], neg_half[:, :],
                                                    ALU.pow).then_inc(a_rstd, 1)
                        if g == 2:
                            pool.wait_ge(a_z, n + 1)
                            nc.gpsimd.tensor_tensor(x_all[:, n, :], x_all[:, n, :], bo[:, :],
                                                    ALU.add).then_inc(a_bo, 1)

            run_batches(pool, 2, 1, self_attention)

            def cross_attention(b, parity, valid):
                n, np_ = b + 1, (parity + 1) % 2
                for g in range(G2):
                    if g == 1 and valid(-1):
                        pool.wait_ge(b_rinv, b)
                        if valid(-2):
                            pool.wait_ge(b_rT, b - 1)
                        pool.sem_inc(alone)
                        nc.gpsimd.tensor_copy(rinv_wide[:, :, :].rearrange("p (a c) e -> p a c e", c=4),
                                              rinv2[:, :].rearrange("p (c a) -> p a c", a=4).unsqueeze(3)
                                              .to_broadcast([P, 4, 4, E2])).then_inc(b_wide, 1)
                    if g == 2 and valid(-2):
                        m = b - 2
                        pool.wait_ge(d_xTe, m + 1)
                        pool.sem_inc(alone)
                        nc.gpsimd.tensor_copy(xnT_hi[:, m, :], xT3[:, :]).then_inc(d_hi, 1)
                        pool.wait_ge(d_hi, m + 1)
                        nc.gpsimd.tensor_tensor(xnT_lo[:, m, :], xT3[:, :], xnT_hi[:, m, :],
                                                ALU.subtract).then_inc(d_cp, 1)
                    if g == 3 and valid(2):
                        pool.wait_ge(b_mv, b + 3)
                        pool.sem_inc(alone)
                        nc.gpsimd.tensor_scalar(ve[:, 2:3], mv[:, 2, 1:2], EPS, None, ALU.add).then_inc(b_ve, 1)
                        pool.wait_ge(b_ve, b + 3)
                        nc.gpsimd.tensor_tensor(rstd[:, 2:3], ve[:, 2:3], neg_half[:, :], ALU.pow).then_inc(b_rstd, 1)
                    if g == 3 and valid(1):
                        pool.wait_ge(b_xn, n + 1)
                        nc.gpsimd.tensor_tensor(x_all[:, n, :], x_all[:, n, :], bp[:, :], ALU.add).then_inc(b_bp, 1)
                    if g == 4 and valid(1):
                        if valid(-1):
                            pool.wait_ge(b_zz, n - 1)
                        dst = vm[:, np_, 0, VPAD:].rearrange("p (h c) -> p h c", c=VGAP)[:, :, 0:E2]
                        src = ctx_row[:, np_, D:2 * D].rearrange("p (h e) -> p h e", e=E2)
                        pool.sem_inc(alone)
                        nc.gpsimd.tensor_copy(dst, src).then_inc(b_vc, 1)
                    if g == 5 and valid(-1):
                        pool.wait_ge(d_mv, b)
                        pool.sem_inc(alone)
                        nc.gpsimd.tensor_scalar(ve[:, 3:4], mv[:, 3, 1:2], EPS, NORM_SCALE ** -2,
                                                ALU.add, ALU.mult).then_inc(d_ve, 1)
                        pool.wait_ge(d_ve, b)
                        nc.gpsimd.tensor_tensor(rstd[:, 3:4], ve[:, 3:4], neg_half[:, :], ALU.pow).then_inc(d_rstd, 1)
                    if g == 6 and valid(2):
                        pool.wait_ge(ld_ctx, 16 * b + 48)
                        if valid(1):
                            pool.wait_ge(b_fill, 3 * b + 4)
                        quad = ctx_row[:, parity, 0:D].rearrange("p (g c) -> p g c", g=4)
                        quad = quad.unsqueeze(2).to_broadcast([P, 4, 2, 32])
                        pool.sem_inc(alone)
                        nc.gpsimd.tensor_copy(keys4[:, :, :, 0, :], quad).then_inc(b_khi, 1)
                        pool.wait_ge(b_khi, b + 3)
                        nc.gpsimd.tensor_tensor(keys4[:, :, :, 1, :], quad, keys4[:, :, :, 0, :],
                                                ALU.subtract).then_inc(b_keys4, 1)

            run_batches(pool, 2, 2, cross_attention)

            for i in range(3 * NE * HT // 4):
                pool.wait_ge(w_staged, i + 1)
                own = slice(4 * (i % 4), 4 * (i % 4) + 4)
                nc.gpsimd.tensor_tensor(w_lo[i // 4][:, own, :], hT[:, i % 2, :].rearrange("p (t q) -> p t q", t=4),
                                        w_hi[i // 4][:, own, :], ALU.subtract).then_inc(w_ev, 1)

            def experts(c, first):
                for e in range(NE):
                    t = NE * c + e
                    pool.wait_ge(f_hi, HT * t + 1)
                    if not (first and e < 2):
                        pool.wait_ge(f_y, t - 1)
                    nc.gpsimd.tensor_tensor(h_lo[:, e % 2, 0, :], hT[:, 0, :], h_hi[:, e % 2, 0, :],
                                            ALU.subtract).then_inc(f_lo0, 1)

            experts(0, True)
            with pool.Fori(1, NC) as c:
                experts(c, False)

        @block.scalar
        def _(act):
            for dst, src in ((bq, b_q), (bk, b_k), (bv, b_v)):
                for a in range(2):
                    act.dma_start(dst[64 * a:64 * a + 64, :],
                                  src.rearrange("(t a) e -> a e t", a=2)[a]).then_inc(ld_b, 16)
            act.dma_start(bo[:, :], b_o.rearrange("(o n) -> o n", o=1).to_broadcast([P, D])).then_inc(ld_b, 16)
            act.dma_start(bp[:, :], b_proj.rearrange("(o n) -> o n", o=1).to_broadcast([P, D])).then_inc(ld_b, 16)
            act.dma_start(lnw[:, :], ln_w.rearrange("(p o) -> p o", o=1)).then_inc(ld_b, 16)
            act.dma_start(lnb[:, :], ln_b.rearrange("(p o) -> p o", o=1)).then_inc(ld_b, 16)
            for i, w in enumerate((wq, wk, wv)):
                act.wait_ge(ld_w[i], 16)
                nc.scalar.activation(w1_hi[:, i, :, :], w[:, :, :], ACT.Copy, scale=W_SCALE).then_inc(w1_hi_done, 1)

            def self_attention(b, parity, valid):
                for g in range(G1):
                    off, u, _ = back(b, parity, g, 3, G1)
                    if valid(off):
                        t = G1 * (b + off) + u
                        act.wait_ge(a_zz, t + 1)
                        if u == 0 and valid(off - 1):
                            act.wait_ge(a_o, b + off)
                        nc.scalar.copy(zT[:, 2 * u:2 * u + 2, :], ps[6][:, 0:2 * P]).then_inc(a_ze, 1)
                    off, u, _ = back(b, parity, g, 2, G1)
                    if valid(off):
                        t = G1 * (b + off) + u
                        act.wait_ge(a_pT, t + 1)
                        nc.scalar.copy(probsT[:, u % 2, :], ps[2 + u % 2][:, :]).then_inc(a_pTe, 1)
                    if valid(0):
                        t = G1 * b + g
                        act.wait_ge(a_max, t + 1)
                        for i in range(HPG):
                            last = nc.scalar.activation(probs[:, g, i * P:(i + 1) * P],
                                                        ps[g % 2][:, i * P:(i + 1) * P], ACT.Exp,
                                                        bias=nmax[:, g, i:i + 1],
                                                        accum_out=rsum[:, g, i:i + 1])
                        last.then_inc(a_exp, 1)
                    if g == 2 and valid(1):
                        n, np_ = b + 1, (parity + 1) % 2
                        for half in range(2):
                            act.wait_ge(a_fill, 6 * n + 5 + half)
                            nc.scalar.activation(v1[:, np_, 512 * half:512 * half + 512], ps[4 + half][:, :], ACT.Copy,
                                                 scale=1.0 / (X1_SCALE * W_SCALE)).then_inc(a_evv, 1)

            run_batches(act, 1, 1, self_attention)

            def cross_attention(b, parity, valid):
                for g in range(G2):
                    off, u, _ = back(b, parity, g, 2, G2)
                    if valid(off) and u not in PT_ON_VECTOR:
                        t = G2 * (b + off) + u
                        act.wait_ge(b_pT, t + 1)
                        nc.scalar.copy(probsT[:, u % 4, :], ps[2 + u % 2][:, :]).then_inc(b_pTa, 1)
                    if valid(0):
                        t = G2 * b + g
                        act.wait_ge(b_max, t + 1)
                        for i in range(2):
                            last = nc.scalar.activation(probs[:, g % 4, i * KEYS2:(i + 1) * KEYS2],
                                                        ps[SCORE_BANKS2[g]][:, i * KEYS2:(i + 1) * KEYS2], ACT.Exp,
                                                        bias=nmax[:, g, i:i + 1],
                                                        accum_out=rsum2[:, parity, 2 * g + i:2 * g + i + 1])
                        last.then_inc(b_exp, 1)
                    if valid(1):
                        n = b + 1
                        if g == 2:
                            act.wait_ge(b_fill, 3 * n + 2)
                            if valid(0):
                                act.wait_ge(b_pack, 3 * n)
                            nc.scalar.copy(q_hi[:, :, :], ps[4][:, :]).then_inc(b_hi, 1)
                        if g == 5:
                            act.wait_ge(b_fill, 3 * n + 3)
                            nc.scalar.copy(k_hi[:, :, :], ps[4][:, :]).then_inc(b_hi, 1)

            run_batches(act, 1, 1, cross_attention)

            act.wait_ge(r_shift, 1)
            nc.scalar.activation(gates[:, :, :], gates[:, :, :], ACT.Exp).then_inc(r_exp, 1)
            for i in range(3 * NE * HT // 4):
                act.wait_ge(raw_T, i + 3)
                nc.scalar.activation(w_hi[i // 4][:, 4 * (i % 4):4 * (i % 4) + 4, :], ps[i % 4][:, :], ACT.Copy,
                                     scale=W_SCALE)
                if i >= 2:
                    act.wait_ge(w_ev, i - 1)
                nc.scalar.activation(hT[:, i % 2, :], ps[i % 4][:, :], ACT.Copy, scale=W_SCALE).then_inc(w_staged, 1)

            def experts(c, first):
                for e in range(NE):
                    for i in range(HT):
                        n = HT * NE * c + HT * e + i
                        act.wait_ge(f_gu, n + 1)
                        if not (first and e == 0):
                            act.wait_ge(f_h, n - 1)
                        nc.scalar.activation(silu[:, i, :], ps[i][:, :], ACT.Silu,
                                             scale=1.0 / (NORM_SCALE * W_SCALE)).then_inc(f_s, 1)
                    for i in range(HT):
                        n = HT * NE * c + HT * e + i
                        act.wait_ge(f_h, n + 1)
                        if not (first and e < 2):
                            act.wait_ge(f_y, NE * c + e - 1)
                        nc.scalar.copy(h_hi[:, e % 2, i, :], hT[:, i, :]).then_inc(f_hi, 1)

            experts(0, True)
            with act.Fori(1, NC) as c:
                experts(c, False)

        @block.vector
        def _(dve):
            nc.vector.memset(qz[:, :, :, :, :], 0.0).then_inc(zeroed, 1)
            nc.vector.memset(vm[:, :, :, :], 0.0).then_inc(zeroed, 1)
            nc.vector.memset(low_q[0:64, :], 0.0)
            nc.vector.memset(low_q[64:P, :], -1.0).then_inc(zeroed, 1)
            for a in range(4):
                last = nc.vector.memset(low_k[32 * a:32 * a + 32, :], -float(a % 2))
            last.then_inc(zeroed, 1)
            dve.wait_ge(c_sel, 9)
            nc.vector.reduce_sum(jmask[:, :], hmask[:, :, :].rearrange("p a j -> p j a"), AX_X).then_inc(zeroed, 1)
            dve.wait_ge(zeroed, 5)
            dve.wait_ge(ld_b, 16 * 10)
            nc.vector.tensor_scalar(bq[:, :], bq[:, :], E1 ** -0.5, None, ALU.mult).then_inc(b1_scaled, 1)
            nc.vector.tensor_scalar(lnw[:, :], lnw[:, :], X1_SCALE, None, ALU.mult).then_inc(b1_scaled, 1)
            nc.vector.tensor_scalar(lnb[:, :], lnb[:, :], X1_SCALE, None, ALU.mult).then_inc(b1_scaled, 1)
            dve.wait_ge(b1_scaled, 3)
            for i, w in enumerate((wq, wk, wv)):
                dve.wait_ge(w1_hi_done, i + 1)
                nc.vector.scalar_tensor_tensor(out=w1_lo[:, i, :, :], in0=w[:, :, :], scalar=W_SCALE,
                                               in1=w1_hi[:, i, :, :], op0=ALU.mult,
                                               op1=ALU.subtract).then_inc(w1_split, 1)
            dve.wait_ge(ld_x0, 16)
            nc.vector.tensor_copy(v1[:, 0, :].rearrange("p (t q) -> p t q", t=PAIRS), bcast(bv[:, :], P)).then_inc(bv_spread, 1)
            dve.wait_ge(raw_T, 1)
            nc.vector.tensor_copy(wqkvT[:, :, :], ps[0][:, 0:3 * P]).then_inc(raw_ev, 1)
            nc.vector.tensor_copy(wprojT[:, :], ps[0][:, 3 * P:4 * P]).then_inc(raw_ev, 1)
            dve.wait_ge(raw_T, 2)
            nc.vector.tensor_scalar(gateT[:, :], ps[1][:, 0:NE], 1.0 / NORM_SCALE, None, ALU.mult).then_inc(raw_ev, 1)
            dve.wait_ge(bvo, 1)
            nc.vector.tensor_tensor(bo[:, :], ps[2][:, 0:P], bo[:, :], ALU.add).then_inc(bo_ready, 1)
            dve.wait_ge(raw_ev, 3)
            for dst, i, f in ((wqR, 0, E2 ** -0.5), (wkR, 1, 1.0)):
                for q4 in range(4):
                    nc.vector.tensor_scalar(dst[:, q4, :, :], wqkvT[:, i, 32 * q4:32 * q4 + 32].unsqueeze(1)
                                            .to_broadcast([P, 4, 32]), f, None, ALU.mult).then_inc(rep_ready, 1)

            def self_attention(b, parity, valid):
                for g in range(G1):
                    if g == 3 and valid(2):
                        dve.wait_ge(a_xT, b + 3)
                        if valid(1):
                            dve.wait_ge(a_xlo, b + 2)
                        nc.vector.tensor_scalar(xT[:, :], ps[7][:, 0:P], lnw[:, :], lnb[:, :],
                                                ALU.mult, ALU.add).then_inc(a_xTe, 1)
                    if valid(0):
                        t = G1 * b + g
                        dve.wait_ge(a_s, t + 1)
                        nc.vector.reduce_max(nmax[:, g, :], ps[g % 2][:, :].rearrange("p (h k) -> p h k", h=HPG),
                                             AX_X, negate=True).then_inc(a_max, 1)
                    off, u, _ = back(b, parity, g, 1, G1)
                    if valid(off):
                        t = G1 * (b + off) + u
                        dve.wait_ge(a_exp, t + 1)
                        nc.vector.reciprocal(rinv[:, u, :], rsum[:, u, :]).then_inc(a_rinv, 1)
                    if valid(1) and g < 2:
                        n, np_ = b + 1, (parity + 1) % 2
                        for half in range(2):
                            dve.wait_ge(a_fill, 6 * n + 2 * g + half + 1)
                            tiles = ps[4 + half][:, :].rearrange("p (t q) -> p t q", t=4)
                            own = slice(4 * half, 4 * half + 4)
                            if g == 0:
                                for a in range(2):
                                    r = slice(64 * a, 64 * a + 64)
                                    last = nc.vector.scalar_tensor_tensor(
                                        out=qz[r, np_, own, a, :], in0=tiles[r],
                                        scalar=E1 ** -0.5 / (X1_SCALE * W_SCALE), in1=bcast(bq[r, own], P),
                                        op0=ALU.mult, op1=ALU.add)
                            else:
                                last = nc.vector.scalar_tensor_tensor(
                                    out=kT[:, np_, own, :], in0=tiles, scalar=1.0 / (X1_SCALE * W_SCALE),
                                    in1=bcast(bk[:, own], P), op0=ALU.mult, op1=ALU.add)
                            last.then_inc(a_evq, 1)
                    if valid(2):
                        n = b + 2
                        if g == 0:
                            src = x_all[:, n, :]
                        if g == 1:
                            dve.wait_ge(a_rstd, 2 * n + 1)
                            nc.vector.tensor_scalar(zln[:, :], x_all[:, n, :], mv[:, 0, 0:1], rstd[:, 0:1],
                                                    ALU.subtract, ALU.mult).then_inc(a_z, 1)
                            dve.wait_ge(a_z, n + 1)
                            src = zln[:, :]
                        if g < 2:
                            dve.sem_inc(alone)
                            nc.vector.bn_stats(bst[:, g, :], src).then_inc(a_bn, 1)
                            dve.wait_ge(a_bn, 2 * n + g + 1)
                            dve.sem_inc(alone)
                            nc.vector.bn_aggr(mv[:, g, :], bst[:, g, :]).then_inc(a_mv, 1)
                        if g == 2:
                            dve.wait_ge(a_rstd, 2 * n + 2)
                            nc.vector.tensor_scalar(xn[:, :], zln[:, :], mv[:, 1, 0:1], rstd[:, 1:2],
                                                    ALU.subtract, ALU.mult).then_inc(a_xn, 1)
                    if g == 3 and valid(-1):
                        n = b - 1
                        dve.wait_ge(a_o, n + 1)
                        dve.wait_ge(a_bo, n + 1)
                        nc.vector.tensor_tensor(x_all[:, n, :], ps[7][:, P:2 * P], x_all[:, n, :],
                                                ALU.add).then_inc(a_res, 1)

            dve.wait_ge(ld_x0, 16)
            dve.wait_ge(ld_x1, 16)
            run_batches(dve, 2, 1, self_attention)

            dve.wait_ge(a_res, NB)

            def pack(dst, hi, bank, low):
                return nc.vector.scalar_tensor_tensor(out=dst, in0=hi, scalar=low[:, :], in1=bank,
                                                      op0=ALU.mult, op1=ALU.add)

            def cross_attention(b, parity, valid):
                n, np_ = b + 1, (parity + 1) % 2
                quads = ps[4][:, :].rearrange("p (g q) -> p g q", g=4)
                for g in range(G2):
                    if g == 1 and valid(-1):
                        dve.wait_ge(b_exp, G2 * b)
                        if valid(-2):
                            dve.wait_ge(b_wide, b - 1)
                        nc.vector.reciprocal(rinv2[:, :], rsum2[:, 1 - parity, :]).then_inc(b_rinv, 1)
                    if g == 1 and valid(1):
                        dve.wait_ge(b_xT, n + 1)
                        nc.vector.tensor_copy(xT2[:, :], ps[7][:, 0:P]).then_inc(b_xTe, 1)
                    if g == 2 and valid(-2):
                        dve.wait_ge(d_xT, b - 1)
                        if valid(-3):
                            dve.wait_ge(d_cp, b - 2)
                        nc.vector.tensor_copy(xT3[:, :], ps[7][:, 2 * P:3 * P]).then_inc(d_xTe, 1)
                    if g == 3 and valid(-2):
                        dve.wait_ge(d_lg, b - 1)
                        nc.vector.tensor_copy(logits[:, b - 2, :], ps[7][:, 3 * P:3 * P + NE]).then_inc(d_lge, 1)
                    if g == 3 and valid(-1):
                        dve.wait_ge(b_rT, b)
                        nc.vector.tensor_copy(rinvT[:, :], ps[7][:, P:2 * P]).then_inc(b_rTe, 1)
                    if g == 7 and valid(1):
                        dve.wait_ge(b_vv, n + 1)
                        dst = vm[:, np_, 1, VPAD:].rearrange("p (h c) -> p h c", c=VGAP)[:, :, 0:E2]
                        nc.vector.tensor_copy(dst, ps[7][:, 0:P].rearrange("p (h e) -> p h e", e=E2)).then_inc(b_vve, 1)
                    if g == 7 and valid(2):
                        dve.wait_ge(b_rstd, b + 3)
                        nc.vector.tensor_scalar(xn2[:, :], x_all[:, b + 2, :], mv[:, 2, 0:1], rstd[:, 2:3],
                                                ALU.subtract, ALU.mult).then_inc(b_xn, 1)
                    if valid(0):
                        dve.wait_ge(b_s, G2 * b + g + 1)
                        nc.vector.reduce_max(nmax[:, g, 0:2], ps[SCORE_BANKS2[g]][:, :].rearrange("p (h k) -> p h k", h=2),
                                             AX_X, negate=True).then_inc(b_max, 1)
                    off, u, _ = back(b, parity, g, 2, G2)
                    if valid(off) and u in PT_ON_VECTOR:
                        dve.wait_ge(b_pT, G2 * (b + off) + u + 1)
                        nc.vector.tensor_copy(probsT[:, u % 4, :], ps[2 + u % 2][:, :]).then_inc(b_pTv, 1)
                    if g == 1 and valid(1):
                        dve.wait_ge(b_fill, 3 * n + 1)
                        nc.vector.tensor_copy(kT2[:, np_, :, 0:P], quads).then_inc(b_pack, 1)
                    if g == 2 and valid(2):
                        dve.sem_inc(alone)
                        nc.vector.bn_stats(bst[:, 2, :], x_all[:, b + 2, :]).then_inc(b_bn, 1)
                        dve.wait_ge(b_bn, b + 3)
                        dve.sem_inc(alone)
                        nc.vector.bn_aggr(mv[:, 2, :], bst[:, 2, :]).then_inc(b_mv, 1)
                    if g == 3 and valid(-1):
                        dve.wait_ge(b_zz, b)
                        dve.wait_ge(b_rTe, b)
                        nc.vector.tensor_tensor(zT2[:, :], ps[6][:, 0:P], rinvT[:, :], ALU.mult).then_inc(b_ze, 1)
                    if g == 3 and valid(1):
                        dve.wait_ge(b_hi, 2 * n + 1)
                        pack(q_part[:, :, :], q_hi[:, :, :], quads, low_q).then_inc(b_pack, 1)
                    if g == 4 and valid(1):
                        dve.wait_ge(b_pack, 3 * n + 2)
                        for j in range(4):
                            nc.vector.tensor_scalar(qm[:, np_, 4 * j:4 * j + 4, :], q_part[:, :, :],
                                                    jmask[:, j:j + 1], None, ALU.mult)
                    if g == 5 and valid(-1):
                        dve.wait_ge(b_pr, b)
                        dve.wait_ge(b_bp, b)
                        nc.vector.tensor_tensor(x_all[:, b - 1, :], ps[7][:, P:2 * P], x_all[:, b - 1, :],
                                                ALU.add).then_inc(b_res, 1)
                        dve.wait_ge(b_res, b)
                        dve.sem_inc(alone)
                        nc.vector.bn_stats(bst[:, 3, :], x_all[:, b - 1, :]).then_inc(d_bn, 1)
                        dve.wait_ge(d_bn, b)
                        dve.sem_inc(alone)
                        nc.vector.bn_aggr(mv[:, 3, :], bst[:, 3, :]).then_inc(d_mv, 1)
                    if g == 6 and valid(1):
                        dve.wait_ge(b_hi, 2 * n + 2)
                        pack(kT2[:, np_, :, P:KEYS2], k_hi[:, :, :], quads, low_k).then_inc(b_pack, 1)
                    if g == 7 and valid(-1):
                        dve.wait_ge(d_rstd, b)
                        nc.vector.tensor_scalar(xn3[:, :], x_all[:, b - 1, :], mv[:, 3, 0:1], rstd[:, 3:4],
                                                ALU.subtract, ALU.mult).then_inc(d_xn, 1)

            run_batches(dve, 2, 2, cross_attention)

            dve.wait_ge(d_lge, NB)
            r_count = [0]

            def then(ins):
                r_count[0] += 1
                ins.then_inc(r_step, 1)
                dve.wait_ge(r_step, r_count[0])

            def over_e(ap):
                return ap.unsqueeze(2).to_broadcast([P, NB, NE])

            rev_b = rev[:, :].unsqueeze(1).to_broadcast([P, NB, NE])
            then(nc.vector.reduce_max(rt_a[:, :], logits[:, :, :], AX_X))
            nc.vector.tensor_tensor(gates[:, :, :], logits[:, :, :], over_e(rt_a[:, :]),
                                    ALU.subtract).then_inc(r_shift, 1)
            dve.wait_ge(r_exp, 1)
            then(nc.vector.reduce_sum(rt_a[:, :], gates[:, :, :], AX_X))
            then(nc.vector.reciprocal(rt_b[:, :], rt_a[:, :]))
            then(nc.vector.tensor_tensor(gates[:, :, :], gates[:, :, :], over_e(rt_b[:, :]), ALU.mult))
            for k in range(TOPK):
                top = topw[:, :, k]
                then(nc.vector.reduce_max(top, gates[:, :, :], AX_X))
                then(nc.vector.tensor_tensor(rt_e[:, :, :], gates[:, :, :], over_e(top), ALU.is_equal))
                then(nc.vector.tensor_tensor(rt_e[:, :, :], rt_e[:, :, :], rev_b, ALU.mult))
                then(nc.vector.reduce_max(rt_a[:, :], rt_e[:, :, :], AX_X))
                then(nc.vector.tensor_tensor(chosen[:, :, k, :], rev_b, over_e(rt_a[:, :]), ALU.is_equal))
                if k == 0:
                    then(nc.vector.scalar_tensor_tensor(out=gates[:, :, :], in0=chosen[:, :, k, :], scalar=-4.0,
                                                        in1=gates[:, :, :], op0=ALU.mult, op1=ALU.add))
            nc.vector.tensor_copy(chosen_b[:, :], chosen[:, :, :, :].rearrange("p b k e -> p (b k e)")).then_inc(r_chosen, 1)
            then(nc.vector.tensor_tensor(rt_a[:, :], topw[:, :, 0], topw[:, :, 1], ALU.add))
            then(nc.vector.tensor_scalar(rt_a[:, :], rt_a[:, :], 1e-9, None, ALU.add))
            then(nc.vector.reciprocal(rt_b[:, :], rt_a[:, :]))
            then(nc.vector.tensor_tensor(topw[:, :, :], topw[:, :, :], bcast(rt_b[:, :], TOPK), ALU.mult))
            dve.wait_ge(r_count_ps, 2)
            then(nc.vector.tensor_copy(scan[:, 0, :], ps[7][:, :]))
            cur, s, kk = 0, 1, TOPK * NE
            while s < NB:
                nc.vector.tensor_copy(scan[:, 1 - cur, 0:s * kk], scan[:, cur, 0:s * kk])
                then(nc.vector.tensor_tensor(scan[:, 1 - cur, s * kk:], scan[:, cur, s * kk:],
                                             scan[:, cur, 0:(NB - s) * kk], ALU.add))
                cur, s = 1 - cur, 2 * s
            ranks = scan[:, cur, :]
            then(nc.vector.tensor_tensor(ranks, ranks, ps[7][:, :], ALU.subtract))
            then(nc.vector.tensor_tensor(ranks, ranks, ps[6][:, :], ALU.add))
            ch = chosen[:, :, :, :].rearrange("p b k e -> p (b k e)")
            then(nc.vector.tensor_scalar(ranks, ranks, float(CAPACITY), None, ALU.is_le))
            then(nc.vector.tensor_tensor(ranks, ranks, ch, ALU.mult))
            rk = ranks.rearrange("p (c e) -> p c e", e=NE)
            then(nc.vector.tensor_tensor(rk, rk, bcast(topw[:, :, :].rearrange("p b k -> p (b k)"), NE), ALU.mult))
            r4 = ranks.rearrange("p (b k e) -> p b k e", k=TOPK, e=NE)
            then(nc.vector.tensor_tensor(comb[:, :, :], r4[:, :, 0, :], r4[:, :, 1, :], ALU.add))
            then(nc.vector.tensor_scalar(comb[:, :, :], comb[:, :, :], 1.0 / (H_SCALE * W_SCALE), None, ALU.mult))

            def add_up(c, e, have_before):
                t = NE * c + e
                dve.wait_ge(f_y, t + 1)
                if have_before:
                    dve.wait_ge(f_acc, t)
                for r in range(CB):
                    n = CB * c + r
                    last = nc.vector.scalar_tensor_tensor(out=x_all[:, n, :], in0=ps[4 + e % 2][:, r * P:(r + 1) * P],
                                                          scalar=comb[:, n, e:e + 1], in1=x_all[:, n, :],
                                                          op0=ALU.mult, op1=ALU.add)
                last.then_inc(f_acc, 1)

            def experts(c, first):
                for e in range(NE):
                    t = NE * c + e
                    for i in range(HT):
                        dve.wait_ge(f_s, HT * t + i + 1)
                        if not (first and e == 0):
                            dve.wait_ge((f_lo0, f_lo1)[i], t)
                        nc.vector.scalar_tensor_tensor(out=hT[:, i, :], in0=ps[2 + i][:, :],
                                                       scalar=H_SCALE / (NORM_SCALE * W_SCALE), in1=silu[:, i, :],
                                                       op0=ALU.mult, op1=ALU.mult).then_inc(f_h, 1)
                    dve.wait_ge(f_hi, HT * t + HT)
                    nc.vector.tensor_tensor(h_lo[:, e % 2, 1, :], hT[:, 1, :], h_hi[:, e % 2, 1, :],
                                            ALU.subtract).then_inc(f_lo1, 1)
                    if e > 0:
                        add_up(c, e - 1, not (first and e == 1))
                    elif not first:
                        add_up(c - 1, NE - 1, True)

            experts(0, True)
            with dve.Fori(1, NC) as c:
                experts(c, False)
            add_up(NC - 1, NE - 1, True)

        @block.tensor
        def _(pe):
            def mm(o, l, r, start=True, stop=True, **kw):
                return nc.tensor.matmul(o, l, r, start=start, stop=stop, **kw)

            pe.wait_ge(c_sel, 9)
            pe.wait_ge(ld_s, 16 * 3)
            for i in range(4):
                last = nc.tensor.transpose(ps[0][:, i * P:(i + 1) * P], raw_s[:, i, :], ident[:, :])
            last.then_inc(raw_T, 1)
            nc.tensor.transpose(ps[1][:, 0:NE], raw_s[0:NE, 4, :], ident[0:NE, 0:NE]).then_inc(raw_T, 1)
            pe.wait_ge(bv_spread, 1)
            pe.wait_ge(ld_wo, 32)
            for i in range(PAIRS):
                last = mm(ps[2][:, 0:P], v1[:, 0, i * P:(i + 1) * P], wo[:, i, :], i == 0, i == PAIRS - 1)
            last.then_inc(bvo, 1)
            pe.wait_ge(bo_ready, 1)
            pe.wait_ge(raw_ev, 3)
            pe.wait_ge(w1_split, 3)
            pe.wait_ge(zeroed, 5)

            def self_attention(b, parity, valid):
                for g in range(G1):
                    if g == 3 and valid(2):
                        pe.wait_ge(a_xn, b + 3)
                        if valid(-2):
                            pe.wait_ge(a_res, b - 1)
                        nc.tensor.transpose(ps[7][:, 0:P], xn[:, :], ident[:, :]).then_inc(a_xT, 1)
                    if valid(0):
                        t = G1 * b + g
                        if g == 0:
                            pe.wait_ge(a_evq, 4 * b + 4)
                        if g >= 2 or valid(-1):
                            pe.wait_ge(a_exp, t - 1)
                        bank = ps[g % 2]
                        mm(bank[:, :], ident_b[:, :], causal[:, :, :].rearrange("p h k -> p (h k)"), True, False)
                        for i in range(HPG):
                            h = HPG * g + i
                            last = mm(bank[:, i * P:(i + 1) * P], qz[:, parity, h // 2, h % 2, :],
                                      kT[:, parity, h // 2, :], False, i == HPG - 1)
                        last.then_inc(a_s, 1)
                    off, u, par = back(b, parity, g, 3, G1)
                    if valid(off):
                        t = G1 * (b + off) + u
                        pe.wait_ge(a_pTe, t + 1)
                        if u == 0:
                            pe.wait_ge(a_evv, 2 * (b + off) + 2)
                        if u > 0 or valid(off - 1):
                            pe.wait_ge(a_ze, t)
                        for i in range(HPG):
                            h = HPG * u + i
                            a = h % 2
                            last = mm(ps[6][64 * a:64 * a + 64, (i // 2) * P:(i // 2 + 1) * P],
                                      v1[:, par, h * E1:(h + 1) * E1], probsT[:, u % 2, i * P:(i + 1) * P])
                        last.then_inc(a_zz, 1)
                    off, u, par = back(b, parity, g, 2, G1)
                    if valid(off):
                        t = G1 * (b + off) + u
                        pe.wait_ge(a_norm, t + 1)
                        if u >= 2 or valid(off - 1):
                            pe.wait_ge(a_pTe, t - 1)
                        for i in range(HPG):
                            last = nc.tensor.transpose(ps[2 + u % 2][:, i * P:(i + 1) * P],
                                                       probs[:, u, i * P:(i + 1) * P], ident[:, :])
                        last.then_inc(a_pT, 1)
                    if g == 3 and valid(-1):
                        n = b - 1
                        pe.wait_ge(a_ze, G1 * n + G1)
                        if valid(2):
                            pe.wait_ge(a_xTe, b + 3)
                        for i in range(PAIRS):
                            last = mm(ps[7][:, P:2 * P], zT[:, i, :], wo[:, i, :], i == 0, i == PAIRS - 1)
                        last.then_inc(a_o, 1)
                    if valid(1) and g < 3:
                        n = b + 1
                        if g == 0:
                            pe.wait_ge(a_xlo, n + 1)
                        for half in range(2):
                            if g == 0 and valid(0):
                                pe.wait_ge(a_evv, 2 * n + half - 1)
                            if g > 0:
                                pe.wait_ge(a_evq, 4 * n + 2 * g + half - 1)
                            parts = ((w1_hi, xT_hi), (w1_hi, xT_lo), (w1_lo, xT_hi))
                            if g < 2:
                                for i in range(4):
                                    pair = 4 * half + i
                                    for k, (w, xs) in enumerate(parts):
                                        last = mm(ps[4 + half][:, i * P:(i + 1) * P],
                                                  w[:, g, 2 * pair:2 * pair + 2, :].rearrange("p h e -> p (h e)"),
                                                  xs[:, :], k == 0, k == 2)
                            else:
                                for k, (w, xs) in enumerate(parts):
                                    last = mm(ps[4 + half][:, :], xs[:, :],
                                              w[:, g, 8 * half:8 * half + 8, :].rearrange("p h e -> p (h e)"),
                                              k == 0, k == 2)
                            last.then_inc(a_fill, 1)

            run_batches(pe, 2, 1, self_attention)
            pe.wait_ge(a_res, NB)
            pe.wait_ge(a_ze, G1 * NB)
            pe.wait_ge(rep_ready, 8)

            def wait_pT(row, u):
                of_vector = len([k for k in PT_ON_VECTOR if k <= u])
                if u in PT_ON_VECTOR:
                    pe.wait_ge(b_pTv, len(PT_ON_VECTOR) * row + of_vector)
                else:
                    pe.wait_ge(b_pTa, (G2 - len(PT_ON_VECTOR)) * row + u + 1 - of_vector)

            def cross_attention(b, parity, valid):
                n = b + 1
                for g in range(G2):
                    if valid(0):
                        t = G2 * b + g
                        if g == 0:
                            pe.wait_ge(b_pack, 3 * b + 3)
                        before = [k for k in range(g) if SCORE_BANKS2[k] == SCORE_BANKS2[g]]
                        lag = g - before[-1] if before else g + G2 - max(k for k in range(G2) if SCORE_BANKS2[k] == SCORE_BANKS2[g])
                        if before or valid(-1):
                            pe.wait_ge(b_exp, t - lag + 1)
                        for i in range(2):
                            last = mm(ps[SCORE_BANKS2[g]][:, i * KEYS2:(i + 1) * KEYS2], qm[:, parity, 2 * g + i, :],
                                      kT2[:, parity, head2(2 * g + i) // 4, :])
                        last.then_inc(b_s, 1)
                    off, u, par = back(b, parity, g, 2, G2)
                    if valid(off):
                        t = G2 * (b + off) + u
                        pe.wait_ge(b_exp, t + 1)
                        if u >= 2 or valid(off - 1):
                            wait_pT(b + off - (u < 2), (u - 2) % G2)
                        for i in range(4):
                            last = nc.tensor.transpose(ps[2 + u % 2][:, i * P:(i + 1) * P],
                                                       probs[:, u % 4, i * P:(i + 1) * P], ident[:, :])
                        last.then_inc(b_pT, 1)
                    off, u, par = back(b, parity, g, 4, G2)
                    if valid(off):
                        wait_pT(b + off, u)
                        if u == 0:
                            pe.wait_ge(b_vc, b + off + 1)
                            pe.wait_ge(b_vve, b + off + 1)
                            if valid(off - 1):
                                pe.wait_ge(b_ze, b + off)
                        for k in range(2):
                            for i in range(2):
                                h = head2(2 * u + i)
                                q4, j = h // 4, h % 4
                                at = VPAD + VGAP * h - E2 * j
                                last = mm(ps[6][32 * q4:32 * q4 + 32, 0:P], vm[:, par, k, at:at + 32],
                                          probsT[:, u % 4, (2 * i + k) * P:(2 * i + k + 1) * P],
                                          j == 0 and k == 0, j == 3 and k == 1)
                        if u == G2 - 1:
                            last.then_inc(b_zz, 1)
                    if g == 0 and valid(1):
                        pe.wait_ge(b_xn, n + 1)
                        if valid(0):
                            pe.wait_ge(b_vve, b + 1)
                        nc.tensor.transpose(ps[7][:, 0:P], xn2[:, :], ident[:, :]).then_inc(b_xT, 1)
                    if g == 1 and valid(-2):
                        pe.wait_ge(d_xn, b - 1)
                        if valid(1):
                            pe.wait_ge(b_xTe, n + 1)
                        nc.tensor.transpose(ps[7][:, 2 * P:3 * P], xn3[:, :], ident[:, :]).then_inc(d_xT, 1)
                    if g == 2 and valid(-1):
                        pe.wait_ge(b_wide, b)
                        if valid(1):
                            pe.wait_ge(b_xTe, n + 1)
                        if valid(-2):
                            pe.wait_ge(d_xTe, b - 1)
                        nc.tensor.transpose(ps[7][:, P:2 * P], rinv_wide[:, :, :].rearrange("p h e -> p (h e)"),
                                            ident[:, :]).then_inc(b_rT, 1)
                    if g == 2 and valid(-2):
                        pe.wait_ge(d_xTe, b - 1)
                        mm(ps[7][:, 3 * P:3 * P + NE], xT3[:, :], gateT[:, :]).then_inc(d_lg, 1)
                    if g == 4 and valid(-1):
                        pe.wait_ge(b_ze, b)
                        if valid(-2):
                            pe.wait_ge(d_lge, b - 1)
                        mm(ps[7][:, P:2 * P], zT2[:, :], wprojT[:, :]).then_inc(b_pr, 1)
                    if g == 0 and valid(1):
                        pe.wait_ge(b_keys4, n + 1)
                        if valid(0):
                            pe.wait_ge(b_pack, 3 * n)
                        for q4 in range(4):
                            last = mm(ps[4][:, q4 * P:(q4 + 1) * P],
                                      keys4[:, q4, :, :, :].rearrange("p a l c -> p (a l c)"), ident_h[:, :])
                        last.then_inc(b_fill, 1)
                    if g in (2, 4) and valid(1):
                        pe.wait_ge(b_xTe, n + 1)
                        pe.wait_ge(b_pack, 3 * n + g // 2)
                        w = wqR if g == 2 else wkR
                        for q4 in range(4):
                            last = mm(ps[4][:, q4 * P:(q4 + 1) * P],
                                      w[:, q4, :, :].rearrange("p a c -> p (a c)"), xT2[:, :])
                        last.then_inc(b_fill, 1)
                    if g == 6 and valid(1):
                        if valid(-1):
                            pe.wait_ge(b_res, b)
                        mm(ps[7][:, 0:P], xT2[:, :], wqkvT[:, 2, :]).then_inc(b_vv, 1)

            run_batches(pe, 1, 2, cross_attention)

            pe.wait_ge(ld_raw, 48)
            pe.wait_ge(d_lge, NB)
            for i in range(3 * NE * HT // 4):
                if i >= 4:
                    pe.wait_ge(w_staged, i - 3)
                for k in range(4):
                    raw = raw_gu[:, 4 * i + k, :] if i < 8 else raw_d[:, 4 * (i - 8) + k, :]
                    last = nc.tensor.transpose(ps[i % 4][:, k * P:(k + 1) * P], raw, ident[:, :])
                last.then_inc(raw_T, 1)
            pe.wait_ge(w_ev, 3 * NE * HT // 4)

            pe.wait_ge(r_chosen, 1)
            pe.wait_ge(d_cp, NB)
            mm(ps[6][:, :], upto[:, :], chosen_b[:, :]).then_inc(r_count_ps, 1)
            mm(ps[7][:, :], ones_b[:, :], chosen_b[:, :]).then_inc(r_count_ps, 1)

            def down(c, e, wait_bank):
                t = NE * c + e
                pe.wait_ge(f_hi, HT * t + HT)
                pe.wait_ge(f_lo0, t + 1)
                pe.wait_ge(f_lo1, t + 1)
                if wait_bank:
                    pe.wait_ge(f_acc, t - 1)
                for r in range(CB):
                    for i in range(HT):
                        own = slice(r * P, (r + 1) * P)
                        w = HT * e + i
                        for k, (h, v) in enumerate(((h_hi, w_hi), (h_hi, w_lo), (h_lo, w_hi))):
                            last = mm(ps[4 + e % 2][:, own], h[:, e % 2, i, own], v[2][:, w, :],
                                      i == 0 and k == 0, i == HT - 1 and k == 2)
                last.then_inc(f_y, 1)

            def experts(c, first):
                own = slice(0, CB) if first else bass.ds(CB * c, CB)
                rows_hi = xnT_hi[:, own, :].rearrange("p b t -> p (b t)")
                rows_lo = xnT_lo[:, own, :].rearrange("p b t -> p (b t)")
                for e in range(NE):
                    for i in range(HT):
                        if not (first and e == 0):
                            pe.wait_ge(f_h, HT * NE * c + HT * e + i - 1)
                        w = HT * e + i
                        for j in range(2):
                            mm(ps[2 * j + i][:, :], w_hi[j][:, w, :], rows_hi, True, False)
                            mm(ps[2 * j + i][:, :], w_hi[j][:, w, :], rows_lo, False, False)
                            last = mm(ps[2 * j + i][:, :], w_lo[j][:, w, :], rows_hi, False, True)
                        last.then_inc(f_gu, 1)
                    if e > 0:
                        down(c, e - 1, not (first and e < 3))
                    elif not first:
                        down(c - 1, NE - 1, True)

            experts(0, True)
            with pe.Fori(1, NC) as c:
                experts(c, False)
            down(NC - 1, NE - 1, True)


_INS = ["x", "ctx_2048", "L0_attn_W_q", "L0_attn_W_k", "L0_attn_W_v", "L0_attn_W_o", "L0_attn_b_q", "L0_attn_b_k",
        "L0_attn_b_v", "L0_attn_b_o", "L0_attn_ln_w", "L0_attn_ln_b", "L0_xattn_w_qkv", "L0_xattn_w_proj",
        "L0_xattn_b_proj", "L0_ffn_gate_w", "L0_ffn_gate_proj_w", "L0_ffn_up_proj_w", "L0_ffn_down_proj_w"]


def kernel(**inputs):
    import numpy as np
    from concourse import bacc
    from concourse.bass_utils import run_bass_kernel_spmd

    nc = bacc.Bacc("TRN2", target_bir_lowering=False, num_devices=1)
    arrays, args = {}, []
    for name in _INS:
        a = np.ascontiguousarray(inputs[name])
        arrays[f"in_{name}"] = a
        args.append(nc.dram_tensor(f"in_{name}", a.shape, mybir.dt.from_np(a.dtype), kind="ExternalInput").ap())
    args.append(nc.dram_tensor("out_x", (NB, P, D), F32, kind="ExternalOutput").ap())
    build(nc, *args)
    return run_bass_kernel_spmd(nc, [arrays], core_ids=[0]).results[0]["out_x"]
```

```python
from contextlib import ExitStack

import concourse.bass as bass
from concourse import mybir

F32 = mybir.dt.float32
BF16 = mybir.dt.bfloat16
F16 = mybir.dt.float16
U32 = mybir.dt.uint32
I32 = mybir.dt.int32
ALU = mybir.AluOpType
ACT = mybir.ActivationFunctionType
AX_X = mybir.AxisListType.X

P = 128
NB = 32
D = 128
H = 16
E1 = 64
PAIRS = H // 2
G1 = 4
HPG = H // G1
E2 = D // H
G2 = 8
KEYS2 = 2 * P
NE = 8
HID = 256
HT = HID // P
TOPK = 2
TOKENS = NB * P
CAPACITY = int(1.25 * TOKENS / NE)
CB = 4
NC = NB // CB
EPS = 1e-5
X1_SCALE = 16.0
NORM_SCALE = 256.0
W_SCALE = 256.0
H_SCALE = 16.0
MASKED = -3.0e38
VGAP = 32
VPAD = VGAP - E2


def head2(n):
    return 4 * (n % 4) + n // 4


PT_ON_VECTOR = (6,)
SCORE_BANKS2 = (0, 1, 5, 0, 1, 5, 0, 1)


def weight_banks(e):
    return ((0, 1), (2, 3))[e] if e < 2 else (6, 7)


def peel(body, b, steps):
    body(b, b % 2, lambda k: 0 <= b + k < NB, steps)


def run_batches(eng, first, last, body, steps, after={}):
    for b in range(first, 3):
        peel(body, b, steps)
        if b in after:
            after[b]()
    with eng.Fori(3, NB - 3, 2) as i:
        body(i, 1, lambda k: True, steps)
        body(i + 1, 0, lambda k: True, steps)
    for b in range(NB - 3, last):
        peel(body, b, steps)


def run_joined(self_attention, cross_attention):
    for b, ahead in ((NB - 2, -2), (NB - 1, -1)):
        for g in range(G1):
            peel(self_attention, b, (g,))
            peel(cross_attention, ahead, (2 * g, 2 * g + 1))
    peel(self_attention, NB, range(G1))


def back(b, parity, g, k, n):
    off, unit = divmod(g - k, n)
    return off, unit, (parity + off) % 2


def build(nc, x, ctx, W_q, W_k, W_v, W_o, b_q, b_k, b_v, b_o, ln_w, ln_b, w_qkv, w_proj, b_proj,
          gate_w, gate_proj_w, up_proj_w, down_proj_w, out):
    es = ExitStack()
    with es:
        def sb(name, shape, dt=F32):
            return es.enter_context(nc.sbuf_tensor(name, shape, dt))

        def sem(name):
            return es.enter_context(nc.semaphore(name))

        es.enter_context(nc.allow_non_contiguous_dma(reason="small weights and biases, loaded once"))

        x_all = sb("x_all", [P, NB, D])
        ctx_row = sb("ctx_row", [P, 2, 2 * D])
        xnT_hi = sb("xnT_hi", [P, NB, P], F16)
        xnT_lo = sb("xnT_lo", [P, NB, P], F16)
        ident = sb("ident", [P, P])
        ident_b = sb("ident_b", [P, P], BF16)
        ident_h = sb("ident_h", [P, P], F16)
        causal = sb("causal", [P, HPG, P], BF16)
        neg_half = sb("neg_half", [P, 1])
        jmask = sb("jmask", [P, 4])
        hmask = sb("hmask", [P, 4, 4])
        low_q = sb("low_q", [P, 1])
        low_k = sb("low_k", [P, 1])

        wq = sb("wq", [P, H, E1])
        wk = sb("wk", [P, H, E1])
        wv = sb("wv", [P, H, E1])
        w1_hi = sb("w1_hi", [P, 3, H, E1], F16)
        w1_lo = sb("w1_lo", [P, 3, H, E1], F16)
        wo = sb("wo", [P, PAIRS, D])
        bq = sb("bq", [P, PAIRS])
        bk = sb("bk", [P, PAIRS])
        bv = sb("bv", [P, PAIRS])
        bo = sb("bo", [P, D])
        bp = sb("bp", [P, D])
        raw_b = sb("raw_b", [PAIRS, 3, P])
        raw_ln = sb("raw_ln", [2, P])
        lnwb = sb("lnwb", [P, 2])

        wqkvT = sb("wqkvT", [P, 3, P])
        wprojT = sb("wprojT", [P, P])
        gateT = sb("gateT", [P, NE])
        w_hi = sb("w_hi", [P, NE, 3 * HT, P], F16)
        w_lo = sb("w_lo", [P, NE, 3 * HT, P], F16)
        upto = sb("upto", [P, P], BF16)
        ones_b = sb("ones_b", [P, P], BF16)
        rev_i = sb("rev_i", [P, NE], I32)
        rev = sb("rev", [P, NE])
        raw_s = sb("raw_s", [P, 5, P])

        qz = sb("qz", [P, 2, PAIRS, 2, P])
        kT = sb("kT", [P, 2, PAIRS, P])
        v1 = sb("v1", [P, 2, H * E1])
        probs = sb("probs", [P, 4, 512])
        probsT = sb("probsT", [P, 4, 512])
        zT = sb("zT", [P, PAIRS, P])
        nmax = sb("nmax", [P, 8, 4])
        rsum = sb("rsum", [P, 8, 4])
        rinv = sb("rinv", [P, 8, 4])
        bst = sb("bst", [P, 4, 6])
        mv = sb("mv", [P, 4, 2])
        ve = sb("ve", [P, 4])
        rstd = sb("rstd", [P, 4])
        zln = sb("zln", [P, D])
        xn = sb("xn", [P, D])
        xT = sb("xT", [P, P])
        xT_hi = sb("xT_hi", [P, P], F16)
        xT_lo = sb("xT_lo", [P, P], F16)

        wqR = sb("wqR", [P, 4, 4, 32])
        wkR = sb("wkR", [P, 4, 4, 32])
        keys4 = sb("keys4", [P, 4, 2, 2, 32], F16)
        q_hi = sb("q_hi", [P, 4, P], F16)
        k_hi = sb("k_hi", [P, 4, P], F16)
        q_part = sb("q_part", [P, 4, P], F16)
        qm = sb("qm", [P, 2, H, P], F16)
        kT2 = sb("kT2", [P, 2, 4, KEYS2], F16)
        vm = sb("vm", [P, 2, 2, VPAD + H * VGAP])
        zT2 = sb("zT2", [P, P])
        rsum2 = sb("rsum2", [P, 2, H])
        rinv2 = sb("rinv2", [P, H])
        rinv_wide = sb("rinv_wide", [P, H, E2])
        rinvT = sb("rinvT", [P, P])
        xn2 = sb("xn2", [P, D])
        xT2 = sb("xT2", [P, P])
        xn3 = sb("xn3", [P, D])
        xT3 = sb("xT3", [P, P])
        logits = sb("logits", [P, NB, NE])
        gates = sb("gates", [P, NB, NE])
        rt_e = sb("rt_e", [P, NB, NE])
        rt_a = sb("rt_a", [P, NB])
        rt_b = sb("rt_b", [P, NB])
        topw = sb("topw", [P, NB, TOPK])
        chosen = sb("chosen", [P, NB, TOPK, NE])
        chosen_b = sb("chosen_b", [P, NB * TOPK * NE], BF16)
        scan = sb("scan", [P, 2, NB * TOPK * NE])
        comb = sb("comb", [P, NB, NE])
        silu = wq[:, :, :].rearrange("p (i h) e -> p i (h e)", i=HT)
        hT = wk[:, :, :].rearrange("p (i h) e -> p i (h e)", i=HT)
        h_hi = sb("h_hi", [P, 2, HT, CB * P], F16)
        h_lo = sb("h_lo", [P, 2, HT, CB * P], F16)
        raw_gu = qz[:, :, :, :, :].rearrange("p a t c q -> p (a t c) q")
        bv_wide = probsT[:, 0:2, :].rearrange("p a q -> p (a q)")
        staged = v1[:, :, 0:3 * HT * P].rearrange("p a (c q) -> p a c q", c=3 * HT)
        raw_d = kT[:, :, :, :].rearrange("p a t q -> p (a t) q")

        ps = [es.enter_context(nc.psum_tensor(f"ps{i}", [P, 512], F32)) for i in range(8)]

        alone = sem("alone")
        c_mem = sem("c_mem"); c_sel = sem("c_sel"); zeroed = sem("zeroed")
        ld_x0 = sem("ld_x0"); ld_x1 = sem("ld_x1"); ld_w = [sem(f"ld_w{i}") for i in range(3)]; ld_wo = sem("ld_wo")
        ld_s = sem("ld_s"); ld_ctx = sem("ld_ctx"); ld_b = sem("ld_b"); ld_ln = sem("ld_ln"); ld_bo = sem("ld_bo"); ln_T = sem("ln_T"); ln_ready = sem("ln_ready"); b1_T = sem("b1_T"); zeroed_q = sem("zeroed_q"); zeroed_v = sem("zeroed_v"); w1_hi_done = sem("w1_hi_done"); w1_split = sem("w1_split"); b1_ready = sem("b1_ready"); bv_spread = sem("bv_spread"); bvo = sem("bvo")
        bo_ready = sem("bo_ready"); rep_ready = sem("rep_ready")
        ld_raw = sem("ld_raw"); raw_T = sem("raw_T"); raw_ev = sem("raw_ev"); w_staged = sem("w_staged"); w_T = sem("w_T"); w_ev = sem("w_ev"); routed = sem("routed");
        a_bn = sem("a_bn"); a_mv = sem("a_mv"); a_ve = sem("a_ve"); a_rstd = sem("a_rstd")
        a_z = sem("a_z"); a_bo = sem("a_bo"); a_xn = sem("a_xn")
        a_xT = sem("a_xT"); a_xTe = sem("a_xTe"); a_xhi = sem("a_xhi"); a_xlo = sem("a_xlo"); a_fill = sem("a_fill"); a_evq = sem("a_evq"); a_evv = sem("a_evv")
        a_s = sem("a_s"); a_max = sem("a_max"); a_exp = sem("a_exp"); a_rinv = sem("a_rinv")
        a_norm = sem("a_norm"); a_pT = sem("a_pT"); a_pTe = sem("a_pTe")
        a_zz = sem("a_zz"); a_ze = sem("a_ze"); a_o = sem("a_o"); a_res = sem("a_res")
        b_bn = sem("b_bn"); b_mv = sem("b_mv"); b_ve = sem("b_ve"); b_rstd = sem("b_rstd")
        b_bp = sem("b_bp"); b_xn = sem("b_xn"); b_vc = sem("b_vc")
        b_xT = sem("b_xT"); b_xTe = sem("b_xTe"); b_fill = sem("b_fill"); b_hi = sem("b_hi"); b_pack = sem("b_pack")
        b_vv = sem("b_vv"); b_vve = sem("b_vve"); b_keys4 = sem("b_keys4"); b_evac = sem("b_evac")
        b_khi = sem("b_khi")
        b_s = sem("b_s"); b_max = sem("b_max"); b_exp = sem("b_exp"); b_rinv = sem("b_rinv")
        b_wide = sem("b_wide"); b_rT = sem("b_rT"); b_rTe = sem("b_rTe")
        b_pT = sem("b_pT"); b_pTa = sem("b_pTa"); b_pTv = sem("b_pTv")
        b_zz = sem("b_zz"); b_ze = sem("b_ze"); b_pr = sem("b_pr"); b_res = sem("b_res")
        d_bn = sem("d_bn"); d_mv = sem("d_mv"); d_ve = sem("d_ve"); d_rstd = sem("d_rstd")
        d_xn = sem("d_xn"); d_xT = sem("d_xT"); d_xTe = sem("d_xTe"); d_hi = sem("d_hi"); d_cp = sem("d_cp")
        d_lg = sem("d_lg"); d_lge = sem("d_lge")
        r_shift = sem("r_shift"); r_exp = sem("r_exp"); r_step = sem("r_step"); r_chosen = sem("r_chosen")
        r_count_ps = sem("r_count_ps")
        f_gu = sem("f_gu"); f_s = sem("f_s"); f_h = sem("f_h"); f_hi = sem("f_hi"); f_lo0 = sem("f_lo0"); f_lo1 = sem("f_lo1"); f_y = sem("f_y"); f_acc = sem("f_acc")
        stored = sem("stored")

        block = es.enter_context(nc.Block())

        out_r = out.rearrange("b t d -> t b d")

        def bcast(ap, n):
            return ap.unsqueeze(2).to_broadcast([ap.shape[0], ap.shape[1], n])

        @block.sync
        def _(sp):
            xr = x.rearrange("b t d -> t b d")
            sp.dma_start(x_all[:, 0:4, :], xr[:, 0:4, :]).then_inc(ld_x0, 16)
            for dst, src, loaded in ((wq, W_q, ld_w[0]), (wk, W_k, ld_w[1]), (wv, W_v, ld_w[2])):
                sp.dma_start(dst[:, :, :], src.rearrange("h d e -> d h e")).then_inc(loaded, 16)
            for a in range(2):
                wo_r = W_o.rearrange("(t a) e d -> a e t d", a=2)
                sp.dma_start(wo[64 * a:64 * a + 64, :, :], wo_r[a]).then_inc(ld_wo, 16)
            sp.dma_start(raw_s[:, 0:3, :], w_qkv.rearrange("(c p) d -> p c d", p=P)).then_inc(ld_s, 16)
            sp.dma_start(raw_s[:, 3, :], w_proj).then_inc(ld_s, 16)
            sp.dma_start(raw_s[0:NE, 4, :], gate_w).then_inc(ld_s, 16)

            sp.dma_start(x_all[:, 4:NB, :], xr[:, 4:NB, :]).then_inc(ld_x1, 16)

            def context(b, parity, valid, steps):
                if valid(1):
                    n, np_ = b + 1, (parity + 1) % 2
                    if valid(0):
                        sp.wait_ge(ld_ctx, 16 * n)
                    if valid(-1):
                        sp.wait_ge(b_keys4, n - 1)
                        sp.wait_ge(b_vc, n - 1)
                    sp.dma_start(ctx_row[:, np_, :], ctx[n, :, :]).then_inc(ld_ctx, 16)

            run_batches(sp, -1, NB - 1, context, None)
            sp.wait_ge(a_zz, G1 * NB)
            sp.dma_start(raw_gu[:, 0:16, :], gate_proj_w.rearrange("e (c p) d -> p (e c) d", p=P)).then_inc(ld_raw, 16)
            sp.dma_start(raw_gu[:, 16:32, :], up_proj_w.rearrange("e (c p) d -> p (e c) d", p=P)).then_inc(ld_raw, 16)
            sp.dma_start(raw_d.rearrange("p (e c) h -> p e (c h)", c=HT),
                         down_proj_w.rearrange("e d h -> d e h")).then_inc(ld_raw, 16)

            for c in range(1):
                sp.wait_ge(f_acc, NE)
                sp.dma_start(out_r[:, 0:CB, :], x_all[:, 0:CB, :]).then_inc(stored, 16)
            with sp.Fori(1, NC) as c:
                sp.wait_ge(f_acc, NE * c + NE)
                sp.dma_start(out_r[:, bass.ds(CB * c, CB), :], x_all[:, bass.ds(CB * c, CB), :]).then_inc(stored, 16)
            sp.wait_ge(stored, 16 * NC)

        @block.gpsimd
        def _(pool):
            nc.gpsimd.memset(ident[:, :], 0.0).then_inc(c_mem, 1)
            nc.gpsimd.memset(causal[:, :, :], 0.0).then_inc(c_mem, 1)
            nc.gpsimd.memset(hmask[:, :, :], 1.0).then_inc(c_mem, 1)
            nc.gpsimd.memset(neg_half[:, :], -0.5).then_inc(c_mem, 1)
            nc.gpsimd.memset(upto[:, :], 1.0).then_inc(c_mem, 1)
            nc.gpsimd.memset(ones_b[:, :], 1.0).then_inc(c_mem, 1)
            pool.wait_ge(c_mem, 6)
            nc.gpsimd.affine_select(out=ident[:, :], in_=ident[:, :], compare_op=ALU.not_equal, fill=1.0,
                                    base=0, pattern=[[-1, P]], channel_multiplier=1).then_inc(c_sel, 1)
            nc.gpsimd.affine_select(out=causal[:, :, :], in_=causal[:, :, :], compare_op=ALU.is_ge,
                                    fill=MASKED, base=0, pattern=[[0, HPG], [-1, P]],
                                    channel_multiplier=1).then_inc(c_sel, 1)
            nc.gpsimd.affine_select(out=hmask[:, :, :], in_=hmask[:, :, :], compare_op=ALU.is_ge, fill=0.0, base=0,
                                    pattern=[[-32, 4], [-E2, 4]], channel_multiplier=1).then_inc(c_sel, 1)
            nc.gpsimd.iota(rev_i[:, :], pattern=[[-1, NE]], base=NE, channel_multiplier=0).then_inc(c_sel, 1)
            nc.gpsimd.affine_select(out=upto[:, :], in_=upto[:, :], compare_op=ALU.is_ge, fill=0.0, base=0,
                                    pattern=[[1, P]], channel_multiplier=-1).then_inc(c_sel, 1)
            pool.wait_ge(c_sel, 5)
            nc.gpsimd.tensor_copy(rev[:, :], rev_i[:, :]).then_inc(c_sel, 1)
            nc.gpsimd.affine_select(out=hmask[:, :, :], in_=hmask[:, :, :], compare_op=ALU.is_ge, fill=0.0, base=E2 - 1,
                                    pattern=[[32, 4], [E2, 4]], channel_multiplier=-1).then_inc(c_sel, 1)
            nc.gpsimd.tensor_copy(ident_b[:, :], ident[:, :]).then_inc(c_sel, 1)
            nc.gpsimd.tensor_copy(ident_h[:, :], ident[:, :]).then_inc(c_sel, 1)


            def self_attention(b, parity, valid, steps):
                for g in steps:
                    if g == 3 and valid(2):
                        n = b + 2
                        pool.wait_ge(a_xTe, n + 1)
                        if valid(1):
                            pool.wait_ge(a_fill, 6 * b + 12)
                        pool.sem_inc(alone)
                        nc.gpsimd.tensor_copy(xT_hi[:, :], xT[:, :]).then_inc(a_xhi, 1)
                        pool.wait_ge(a_xhi, n + 1)
                        nc.gpsimd.tensor_tensor(xT_lo[:, :], xT[:, :], xT_hi[:, :], ALU.subtract).then_inc(a_xlo, 1)
                    off, u, _ = back(b, parity, g, 1, G1)
                    if valid(off):
                        t = G1 * (b + off) + u
                        pool.wait_ge(a_rinv, t + 1)
                        pr = probs[:, u, :].rearrange("p (h k) -> p h k", h=HPG)
                        nc.gpsimd.tensor_tensor(pr, pr, bcast(rinv[:, u, :], P), ALU.mult).then_inc(a_norm, 1)
                    if valid(2):
                        n = b + 2
                        if g < 2:
                            pool.wait_ge(a_mv, 2 * n + g + 1)
                            pool.sem_inc(alone)
                            nc.gpsimd.tensor_scalar(ve[:, g:g + 1], mv[:, g, 1:2], EPS, None,
                                                    ALU.add).then_inc(a_ve, 1)
                            pool.wait_ge(a_ve, 2 * n + g + 1)
                            nc.gpsimd.tensor_tensor(rstd[:, g:g + 1], ve[:, g:g + 1], neg_half[:, :],
                                                    ALU.pow).then_inc(a_rstd, 1)
                    if valid(0) and g == 3:
                        if not valid(-1):
                            pool.wait_ge(bo_ready, 1)
                        pool.wait_ge(a_z, b + 1)
                        nc.gpsimd.tensor_tensor(x_all[:, b, :], x_all[:, b, :], bo[:, :], ALU.add).then_inc(a_bo, 1)

            def cross_attention(b, parity, valid, steps):
                n, np_ = b + 1, (parity + 1) % 2
                for g in steps:
                    if g == 1 and valid(-1):
                        pool.wait_ge(b_rinv, b)
                        if valid(-2):
                            pool.wait_ge(b_rT, b - 1)
                        pool.sem_inc(alone)
                        nc.gpsimd.tensor_copy(rinv_wide[:, :, :].rearrange("p (a c) e -> p a c e", c=4),
                                              rinv2[:, :].rearrange("p (c a) -> p a c", a=4).unsqueeze(3)
                                              .to_broadcast([P, 4, 4, E2])).then_inc(b_wide, 1)
                    if g == 2 and valid(-2):
                        m = b - 2
                        pool.wait_ge(d_xTe, m + 1)
                        pool.sem_inc(alone)
                        nc.gpsimd.tensor_copy(xnT_hi[:, m, :], xT3[:, :]).then_inc(d_hi, 1)
                        pool.wait_ge(d_hi, m + 1)
                        nc.gpsimd.tensor_tensor(xnT_lo[:, m, :], xT3[:, :], xnT_hi[:, m, :],
                                                ALU.subtract).then_inc(d_cp, 1)
                    if g == 3 and valid(2):
                        pool.wait_ge(b_mv, b + 3)
                        pool.sem_inc(alone)
                        nc.gpsimd.tensor_scalar(ve[:, 2:3], mv[:, 2, 1:2], EPS, None, ALU.add).then_inc(b_ve, 1)
                        pool.wait_ge(b_ve, b + 3)
                        nc.gpsimd.tensor_tensor(rstd[:, 2:3], ve[:, 2:3], neg_half[:, :], ALU.pow).then_inc(b_rstd, 1)
                    if g == 3 and valid(1):
                        pool.wait_ge(b_xn, n + 1)
                        nc.gpsimd.tensor_tensor(x_all[:, n, :], x_all[:, n, :], bp[:, :], ALU.add).then_inc(b_bp, 1)
                    if g == 4 and valid(1):
                        if valid(-1):
                            pool.wait_ge(b_zz, n - 1)
                        dst = vm[:, np_, 0, VPAD:].rearrange("p (h c) -> p h c", c=VGAP)[:, :, 0:E2]
                        src = ctx_row[:, np_, D:2 * D].rearrange("p (h e) -> p h e", e=E2)
                        pool.sem_inc(alone)
                        nc.gpsimd.tensor_copy(dst, src).then_inc(b_vc, 1)
                    if g == 5 and valid(-1):
                        pool.wait_ge(d_mv, b)
                        pool.sem_inc(alone)
                        nc.gpsimd.tensor_scalar(ve[:, 3:4], mv[:, 3, 1:2], EPS, NORM_SCALE ** -2,
                                                ALU.add, ALU.mult).then_inc(d_ve, 1)
                        pool.wait_ge(d_ve, b)
                        nc.gpsimd.tensor_tensor(rstd[:, 3:4], ve[:, 3:4], neg_half[:, :], ALU.pow).then_inc(d_rstd, 1)
                    if g == 6 and valid(2):
                        pool.wait_ge(ld_ctx, 16 * b + 48)
                        if valid(1):
                            pool.wait_ge(b_fill, 3 * b + 4)
                        quad = ctx_row[:, parity, 0:D].rearrange("p (g c) -> p g c", g=4)
                        quad = quad.unsqueeze(2).to_broadcast([P, 4, 2, 32])
                        pool.sem_inc(alone)
                        nc.gpsimd.tensor_copy(keys4[:, :, :, 0, :], quad).then_inc(b_khi, 1)
                        pool.wait_ge(b_khi, b + 3)
                        nc.gpsimd.tensor_tensor(keys4[:, :, :, 1, :], quad, keys4[:, :, :, 0, :],
                                                ALU.subtract).then_inc(b_keys4, 1)

            def prepare():
                nc.gpsimd.memset(vm[:, :, :, :], 0.0).then_inc(zeroed_v, 1)
                pool.wait_ge(zeroed_v, 1)
                pool.wait_ge(ld_bo, 32)

            run_batches(pool, -2, NB - 2, self_attention, range(G1), {-2: prepare})
            run_joined(self_attention, cross_attention)
            run_batches(pool, 0, NB + 2, cross_attention, range(G2))

            def split_weights(e):
                pool.wait_ge(w_staged, e + 1)
                nc.gpsimd.tensor_tensor(w_lo[:, e, :, :], staged[:, e % 2, :, :], w_hi[:, e, :, :],
                                        ALU.subtract).then_inc(w_ev, 1)

            split_weights(0)
            split_weights(1)

            def experts(c, first):
                for e in range(NE):
                    t = NE * c + e
                    pool.wait_ge(f_hi, HT * t + 1)
                    if not (first and e < 2):
                        pool.wait_ge(f_y, t - 1)
                    nc.gpsimd.tensor_tensor(h_lo[:, e % 2, 0, :], hT[:, 0, :], h_hi[:, e % 2, 0, :],
                                            ALU.subtract).then_inc(f_lo0, 1)
                    if first and e + 2 < NE:
                        split_weights(e + 2)

            experts(0, True)
            with pool.Fori(1, NC) as c:
                experts(c, False)

        @block.scalar
        def _(act):
            act.dma_start(raw_ln[0:1, :], ln_w.rearrange("(o n) -> o n", o=1)).then_inc(ld_ln, 16)
            act.dma_start(raw_ln[1:2, :], ln_b.rearrange("(o n) -> o n", o=1)).then_inc(ld_ln, 16)
            for i, src in enumerate((b_q, b_k, b_v)):
                act.dma_start(raw_b[:, i, :], src.rearrange("(t a) e -> t (a e)", a=2)).then_inc(ld_b, 16)
            act.dma_start(bo[:, :], b_o.rearrange("(o n) -> o n", o=1).to_broadcast([P, D])).then_inc(ld_bo, 16)
            act.dma_start(bp[:, :], b_proj.rearrange("(o n) -> o n", o=1).to_broadcast([P, D])).then_inc(ld_bo, 16)
            for i, w in enumerate((wq, wk, wv)):
                act.wait_ge(ld_w[i], 16)
                nc.scalar.activation(w1_hi[:, i, :, :], w[:, :, :], ACT.Copy, scale=W_SCALE).then_inc(w1_hi_done, 1)

            def self_attention(b, parity, valid, steps):
                for g in steps:
                    off, u, _ = back(b, parity, g, 3, G1)
                    if valid(off):
                        t = G1 * (b + off) + u
                        act.wait_ge(a_zz, t + 1)
                        if u == 0 and valid(off - 1):
                            act.wait_ge(a_o, b + off)
                        nc.scalar.copy(zT[:, 2 * u:2 * u + 2, :], ps[6][:, 0:2 * P]).then_inc(a_ze, 1)
                    off, u, _ = back(b, parity, g, 2, G1)
                    if valid(off):
                        t = G1 * (b + off) + u
                        act.wait_ge(a_pT, t + 1)
                        nc.scalar.copy(probsT[:, u % 2, :], ps[2 + u % 2][:, :]).then_inc(a_pTe, 1)
                    if valid(0):
                        t = G1 * b + g
                        act.wait_ge(a_max, t + 1)
                        for i in range(HPG):
                            last = nc.scalar.activation(probs[:, g, i * P:(i + 1) * P],
                                                        ps[g % 2][:, i * P:(i + 1) * P], ACT.Exp,
                                                        bias=nmax[:, g, i:i + 1],
                                                        accum_out=rsum[:, g, i:i + 1])
                        last.then_inc(a_exp, 1)
                    if g == 2 and valid(1):
                        n, np_ = b + 1, (parity + 1) % 2
                        for half in range(2):
                            act.wait_ge(a_fill, 6 * n + 5 + half)
                            nc.scalar.activation(v1[:, np_, 512 * half:512 * half + 512], ps[4 + half][:, :], ACT.Copy,
                                                 scale=1.0 / (X1_SCALE * W_SCALE)).then_inc(a_evv, 1)

            def cross_attention(b, parity, valid, steps):
                for g in steps:
                    off, u, _ = back(b, parity, g, 2, G2)
                    if valid(off) and u not in PT_ON_VECTOR:
                        t = G2 * (b + off) + u
                        act.wait_ge(b_pT, t + 1)
                        nc.scalar.copy(probsT[:, u % 4, :], ps[2 + u % 2][:, :]).then_inc(b_pTa, 1)
                    if valid(0):
                        t = G2 * b + g
                        act.wait_ge(b_max, t + 1)
                        for i in range(2):
                            last = nc.scalar.activation(probs[:, g % 4, i * KEYS2:(i + 1) * KEYS2],
                                                        ps[SCORE_BANKS2[g]][:, i * KEYS2:(i + 1) * KEYS2], ACT.Exp,
                                                        bias=nmax[:, g, i:i + 1],
                                                        accum_out=rsum2[:, parity, 2 * g + i:2 * g + i + 1])
                        last.then_inc(b_exp, 1)
                    if valid(1):
                        n = b + 1
                        if g == 2:
                            act.wait_ge(b_fill, 3 * n + 2)
                            if valid(0):
                                act.wait_ge(b_pack, 3 * n)
                            nc.scalar.copy(q_hi[:, :, :], ps[4][:, :]).then_inc(b_hi, 1)
                        if g == 5:
                            act.wait_ge(b_fill, 3 * n + 3)
                            nc.scalar.copy(k_hi[:, :, :], ps[4][:, :]).then_inc(b_hi, 1)

            run_batches(act, -1, NB - 2, self_attention, range(G1))
            run_joined(self_attention, cross_attention)
            run_batches(act, 0, NB + 1, cross_attention, range(G2))

            act.wait_ge(r_shift, 1)
            nc.scalar.activation(gates[:, :, :], gates[:, :, :], ACT.Exp).then_inc(r_exp, 1)
            def take_weights(e):
                act.wait_ge(w_T, e + 1)
                if e >= 2:
                    act.wait_ge(w_ev, e - 1)
                for k, tiles in enumerate((slice(0, 2 * HT), slice(2 * HT, 3 * HT))):
                    bank = ps[weight_banks(e)[k]][:, 0:(tiles.stop - tiles.start) * P]
                    nc.scalar.activation(w_hi[:, e, tiles, :], bank, ACT.Copy, scale=W_SCALE)
                    last = nc.scalar.activation(staged[:, e % 2, tiles, :], bank, ACT.Copy, scale=W_SCALE)
                last.then_inc(w_staged, 1)

            take_weights(0)
            take_weights(1)

            def experts(c, first):
                for e in range(NE):
                    for i in range(HT):
                        n = HT * NE * c + HT * e + i
                        act.wait_ge(f_gu, n + 1)
                        if not (first and e == 0):
                            act.wait_ge(f_h, n - 1)
                        nc.scalar.activation(silu[:, i, :], ps[i][:, :], ACT.Silu,
                                             scale=1.0 / (NORM_SCALE * W_SCALE)).then_inc(f_s, 1)
                    for i in range(HT):
                        n = HT * NE * c + HT * e + i
                        act.wait_ge(f_h, n + 1)
                        if not (first and e < 2):
                            act.wait_ge(f_y, NE * c + e - 1)
                        nc.scalar.copy(h_hi[:, e % 2, i, :], hT[:, i, :]).then_inc(f_hi, 1)
                    if first and e + 2 < NE:
                        take_weights(e + 2)

            experts(0, True)
            with act.Fori(1, NC) as c:
                experts(c, False)

        @block.vector
        def _(dve):
            nc.vector.memset(qz[:, :, :, :, :], 0.0).then_inc(zeroed_q, 1)
            dve.wait_ge(ln_T, 1)
            nc.vector.tensor_scalar(lnwb[:, :], ps[1][:, 0:2], X1_SCALE, None, ALU.mult).then_inc(ln_ready, 1)
            dve.wait_ge(ln_ready, 1)

            def self_attention(b, parity, valid, steps):
                for g in steps:
                    if g == 3 and valid(2):
                        dve.wait_ge(a_xT, b + 3)
                        if valid(1):
                            dve.wait_ge(a_xlo, b + 2)
                        nc.vector.tensor_scalar(xT[:, :], ps[7][:, 0:P], lnwb[:, 0:1], lnwb[:, 1:2],
                                                ALU.mult, ALU.add).then_inc(a_xTe, 1)
                    if valid(0):
                        t = G1 * b + g
                        dve.wait_ge(a_s, t + 1)
                        nc.vector.reduce_max(nmax[:, g, :], ps[g % 2][:, :].rearrange("p (h k) -> p h k", h=HPG),
                                             AX_X, negate=True).then_inc(a_max, 1)
                    off, u, _ = back(b, parity, g, 1, G1)
                    if valid(off):
                        t = G1 * (b + off) + u
                        dve.wait_ge(a_exp, t + 1)
                        nc.vector.reciprocal(rinv[:, u, :], rsum[:, u, :]).then_inc(a_rinv, 1)
                    if valid(1) and g < 2:
                        n, np_ = b + 1, (parity + 1) % 2
                        for half in range(2):
                            dve.wait_ge(a_fill, 6 * n + 2 * g + half + 1)
                            tiles = ps[4 + half][:, :].rearrange("p (t q) -> p t q", t=4)
                            own = slice(4 * half, 4 * half + 4)
                            if g == 0:
                                for a in range(2):
                                    r = slice(64 * a, 64 * a + 64)
                                    last = nc.vector.scalar_tensor_tensor(
                                        out=qz[r, np_, own, a, :], in0=tiles[r],
                                        scalar=E1 ** -0.5 / (X1_SCALE * W_SCALE), in1=bcast(bq[r, own], P),
                                        op0=ALU.mult, op1=ALU.add)
                            else:
                                last = nc.vector.scalar_tensor_tensor(
                                    out=kT[:, np_, own, :], in0=tiles, scalar=1.0 / (X1_SCALE * W_SCALE),
                                    in1=bcast(bk[:, own], P), op0=ALU.mult, op1=ALU.add)
                            last.then_inc(a_evq, 1)
                    if valid(2):
                        n = b + 2
                        if g == 0:
                            if valid(-2) and not valid(-3):
                                dve.wait_ge(ld_x1, 16)
                            src = x_all[:, n, :]
                        if g == 1:
                            dve.wait_ge(a_rstd, 2 * n + 1)
                            nc.vector.tensor_scalar(zln[:, :], x_all[:, n, :], mv[:, 0, 0:1], rstd[:, 0:1],
                                                    ALU.subtract, ALU.mult).then_inc(a_z, 1)
                            dve.wait_ge(a_z, n + 1)
                            src = zln[:, :]
                        if g < 2:
                            dve.sem_inc(alone)
                            nc.vector.bn_stats(bst[:, g, :], src).then_inc(a_bn, 1)
                            dve.wait_ge(a_bn, 2 * n + g + 1)
                            dve.sem_inc(alone)
                            nc.vector.bn_aggr(mv[:, g, :], bst[:, g, :]).then_inc(a_mv, 1)
                        if g == 2:
                            dve.wait_ge(a_rstd, 2 * n + 2)
                            nc.vector.tensor_scalar(xn[:, :], zln[:, :], mv[:, 1, 0:1], rstd[:, 1:2],
                                                    ALU.subtract, ALU.mult).then_inc(a_xn, 1)
                    if g == 3 and valid(-1):
                        n = b - 1
                        dve.wait_ge(a_o, n + 1)
                        dve.wait_ge(a_bo, n + 1)
                        nc.vector.tensor_tensor(x_all[:, n, :], ps[7][:, P:2 * P], x_all[:, n, :],
                                                ALU.add).then_inc(a_res, 1)

            def prepare():
                dve.wait_ge(b1_T, 1)
                nc.vector.tensor_scalar(bq[:, :], ps[1][:, 0:PAIRS], E1 ** -0.5, None, ALU.mult)
                nc.vector.tensor_copy(bk[:, :], ps[1][:, PAIRS:2 * PAIRS])
                nc.vector.tensor_copy(bv[:, :], ps[1][:, 2 * PAIRS:3 * PAIRS]).then_inc(b1_ready, 1)
                dve.wait_ge(b1_ready, 1)
                dve.wait_ge(zeroed_q, 1)
                for i, w in enumerate((wq, wk, wv)):
                    dve.wait_ge(w1_hi_done, i + 1)
                    nc.vector.scalar_tensor_tensor(out=w1_lo[:, i, :, :], in0=w[:, :, :], scalar=W_SCALE,
                                                   in1=w1_hi[:, i, :, :], op0=ALU.mult,
                                                   op1=ALU.subtract).then_inc(w1_split, 1)

            def prepare_cross():
                nc.vector.tensor_copy(bv_wide.rearrange("p (t q) -> p t q", t=PAIRS),
                                      bcast(bv[:, :], P)).then_inc(bv_spread, 1)
                dve.wait_ge(raw_T, 1)
                nc.vector.tensor_copy(wqkvT[:, :, :], ps[3][:, 0:3 * P]).then_inc(raw_ev, 1)
                nc.vector.tensor_copy(wprojT[:, :], ps[3][:, 3 * P:4 * P]).then_inc(raw_ev, 1)
                dve.wait_ge(raw_ev, 2)
                for dst, i, f in ((wqR, 0, E2 ** -0.5), (wkR, 1, 1.0)):
                    for q4 in range(4):
                        nc.vector.tensor_scalar(dst[:, q4, :, :], wqkvT[:, i, 32 * q4:32 * q4 + 32].unsqueeze(1)
                                                .to_broadcast([P, 4, 32]), f, None, ALU.mult).then_inc(rep_ready, 1)
                dve.wait_ge(bvo, 1)
                dve.wait_ge(ld_bo, 32)
                nc.vector.tensor_scalar(gateT[:, :], ps[6][:, P:P + NE], 1.0 / NORM_SCALE, None,
                                        ALU.mult).then_inc(raw_ev, 1)
                nc.vector.tensor_tensor(bo[:, :], ps[6][:, 0:P], bo[:, :], ALU.add).then_inc(bo_ready, 1)
                nc.vector.memset(low_q[0:64, :], 0.0)
                nc.vector.memset(low_q[64:P, :], -1.0).then_inc(zeroed, 1)
                for a in range(4):
                    last = nc.vector.memset(low_k[32 * a:32 * a + 32, :], -float(a % 2))
                last.then_inc(zeroed, 1)
                dve.wait_ge(c_sel, 9)
                nc.vector.reduce_sum(jmask[:, :], hmask[:, :, :].rearrange("p a j -> p j a"), AX_X).then_inc(zeroed, 1)
                dve.wait_ge(zeroed, 3)
                dve.wait_ge(zeroed_v, 1)

            def pack(dst, hi, bank, low):
                return nc.vector.scalar_tensor_tensor(out=dst, in0=hi, scalar=low[:, :], in1=bank,
                                                      op0=ALU.mult, op1=ALU.add)

            def cross_attention(b, parity, valid, steps):
                n, np_ = b + 1, (parity + 1) % 2
                quads = ps[4][:, :].rearrange("p (g q) -> p g q", g=4)
                for g in steps:
                    if g == 1 and valid(-1):
                        dve.wait_ge(b_exp, G2 * b)
                        if valid(-2):
                            dve.wait_ge(b_wide, b - 1)
                        nc.vector.reciprocal(rinv2[:, :], rsum2[:, 1 - parity, :]).then_inc(b_rinv, 1)
                    if g == 1 and valid(1):
                        dve.wait_ge(b_xT, n + 1)
                        nc.vector.tensor_copy(xT2[:, :], ps[7][:, 0:P]).then_inc(b_xTe, 1)
                    if g == 2 and valid(-2):
                        dve.wait_ge(d_xT, b - 1)
                        if valid(-3):
                            dve.wait_ge(d_cp, b - 2)
                        nc.vector.tensor_copy(xT3[:, :], ps[7][:, 2 * P:3 * P]).then_inc(d_xTe, 1)
                    if g == 3 and valid(-2):
                        dve.wait_ge(d_lg, b - 1)
                        nc.vector.tensor_copy(logits[:, b - 2, :], ps[7][:, 3 * P:3 * P + NE]).then_inc(d_lge, 1)
                    if g == 3 and valid(-1):
                        dve.wait_ge(b_rT, b)
                        nc.vector.tensor_copy(rinvT[:, :], ps[7][:, P:2 * P]).then_inc(b_rTe, 1)
                    if g == 7 and valid(1):
                        dve.wait_ge(b_vv, n + 1)
                        dst = vm[:, np_, 1, VPAD:].rearrange("p (h c) -> p h c", c=VGAP)[:, :, 0:E2]
                        nc.vector.tensor_copy(dst, ps[7][:, 0:P].rearrange("p (h e) -> p h e", e=E2)).then_inc(b_vve, 1)
                    if g == 7 and valid(2):
                        dve.wait_ge(b_rstd, b + 3)
                        nc.vector.tensor_scalar(xn2[:, :], x_all[:, b + 2, :], mv[:, 2, 0:1], rstd[:, 2:3],
                                                ALU.subtract, ALU.mult).then_inc(b_xn, 1)
                    if valid(0):
                        dve.wait_ge(b_s, G2 * b + g + 1)
                        nc.vector.reduce_max(nmax[:, g, 0:2], ps[SCORE_BANKS2[g]][:, :].rearrange("p (h k) -> p h k", h=2),
                                             AX_X, negate=True).then_inc(b_max, 1)
                    off, u, _ = back(b, parity, g, 2, G2)
                    if valid(off) and u in PT_ON_VECTOR:
                        dve.wait_ge(b_pT, G2 * (b + off) + u + 1)
                        nc.vector.tensor_copy(probsT[:, u % 4, :], ps[2 + u % 2][:, :]).then_inc(b_pTv, 1)
                    if g == 1 and valid(1):
                        dve.wait_ge(b_fill, 3 * n + 1)
                        nc.vector.tensor_copy(kT2[:, np_, :, 0:P], quads).then_inc(b_pack, 1)
                    if g == 2 and valid(2):
                        dve.sem_inc(alone)
                        nc.vector.bn_stats(bst[:, 2, :], x_all[:, b + 2, :]).then_inc(b_bn, 1)
                        dve.wait_ge(b_bn, b + 3)
                        dve.sem_inc(alone)
                        nc.vector.bn_aggr(mv[:, 2, :], bst[:, 2, :]).then_inc(b_mv, 1)
                    if g == 3 and valid(-1):
                        dve.wait_ge(b_zz, b)
                        dve.wait_ge(b_rTe, b)
                        nc.vector.tensor_tensor(zT2[:, :], ps[6][:, 0:P], rinvT[:, :], ALU.mult).then_inc(b_ze, 1)
                    if g == 3 and valid(1):
                        dve.wait_ge(b_hi, 2 * n + 1)
                        pack(q_part[:, :, :], q_hi[:, :, :], quads, low_q).then_inc(b_pack, 1)
                    if g == 4 and valid(1):
                        dve.wait_ge(b_pack, 3 * n + 2)
                        for j in range(4):
                            nc.vector.tensor_scalar(qm[:, np_, 4 * j:4 * j + 4, :], q_part[:, :, :],
                                                    jmask[:, j:j + 1], None, ALU.mult)
                    if g == 5 and valid(-1):
                        dve.wait_ge(b_pr, b)
                        dve.wait_ge(b_bp, b)
                        nc.vector.tensor_tensor(x_all[:, b - 1, :], ps[7][:, P:2 * P], x_all[:, b - 1, :],
                                                ALU.add).then_inc(b_res, 1)
                        dve.wait_ge(b_res, b)
                        dve.sem_inc(alone)
                        nc.vector.bn_stats(bst[:, 3, :], x_all[:, b - 1, :]).then_inc(d_bn, 1)
                        dve.wait_ge(d_bn, b)
                        dve.sem_inc(alone)
                        nc.vector.bn_aggr(mv[:, 3, :], bst[:, 3, :]).then_inc(d_mv, 1)
                    if g == 6 and valid(1):
                        dve.wait_ge(b_hi, 2 * n + 2)
                        pack(kT2[:, np_, :, P:KEYS2], k_hi[:, :, :], quads, low_k).then_inc(b_pack, 1)
                    if g == 7 and valid(-1):
                        dve.wait_ge(d_rstd, b)
                        nc.vector.tensor_scalar(xn3[:, :], x_all[:, b - 1, :], mv[:, 3, 0:1], rstd[:, 3:4],
                                                ALU.subtract, ALU.mult).then_inc(d_xn, 1)

            dve.wait_ge(ld_x0, 16)
            run_batches(dve, -2, NB - 2, self_attention, range(G1), {-2: prepare, -1: prepare_cross})
            dve.wait_ge(a_res, NB - 3)
            run_joined(self_attention, cross_attention)
            dve.wait_ge(a_res, NB)
            run_batches(dve, 0, NB + 2, cross_attention, range(G2))

            dve.wait_ge(d_lge, NB)
            r_count = [0]

            def then(ins):
                r_count[0] += 1
                ins.then_inc(r_step, 1)
                dve.wait_ge(r_step, r_count[0])

            def over_e(ap):
                return ap.unsqueeze(2).to_broadcast([P, NB, NE])

            rev_b = rev[:, :].unsqueeze(1).to_broadcast([P, NB, NE])
            then(nc.vector.reduce_max(rt_a[:, :], logits[:, :, :], AX_X))
            nc.vector.tensor_tensor(gates[:, :, :], logits[:, :, :], over_e(rt_a[:, :]),
                                    ALU.subtract).then_inc(r_shift, 1)
            dve.wait_ge(r_exp, 1)
            then(nc.vector.reduce_sum(rt_a[:, :], gates[:, :, :], AX_X))
            then(nc.vector.reciprocal(rt_b[:, :], rt_a[:, :]))
            then(nc.vector.tensor_tensor(gates[:, :, :], gates[:, :, :], over_e(rt_b[:, :]), ALU.mult))
            for k in range(TOPK):
                top = topw[:, :, k]
                then(nc.vector.reduce_max(top, gates[:, :, :], AX_X))
                then(nc.vector.tensor_tensor(rt_e[:, :, :], gates[:, :, :], over_e(top), ALU.is_equal))
                then(nc.vector.tensor_tensor(rt_e[:, :, :], rt_e[:, :, :], rev_b, ALU.mult))
                then(nc.vector.reduce_max(rt_a[:, :], rt_e[:, :, :], AX_X))
                then(nc.vector.tensor_tensor(chosen[:, :, k, :], rev_b, over_e(rt_a[:, :]), ALU.is_equal))
                if k == 0:
                    then(nc.vector.scalar_tensor_tensor(out=gates[:, :, :], in0=chosen[:, :, k, :], scalar=-4.0,
                                                        in1=gates[:, :, :], op0=ALU.mult, op1=ALU.add))
            nc.vector.tensor_copy(chosen_b[:, :], chosen[:, :, :, :].rearrange("p b k e -> p (b k e)")).then_inc(r_chosen, 1)
            then(nc.vector.tensor_tensor(rt_a[:, :], topw[:, :, 0], topw[:, :, 1], ALU.add))
            then(nc.vector.tensor_scalar(rt_a[:, :], rt_a[:, :], 1e-9, None, ALU.add))
            then(nc.vector.reciprocal(rt_b[:, :], rt_a[:, :]))
            then(nc.vector.tensor_tensor(topw[:, :, :], topw[:, :, :], bcast(rt_b[:, :], TOPK), ALU.mult))
            dve.wait_ge(r_count_ps, 2)
            then(nc.vector.tensor_copy(scan[:, 0, :], ps[7][:, :]))
            cur, s, kk = 0, 1, TOPK * NE
            while s < NB:
                nc.vector.tensor_copy(scan[:, 1 - cur, 0:s * kk], scan[:, cur, 0:s * kk])
                then(nc.vector.tensor_tensor(scan[:, 1 - cur, s * kk:], scan[:, cur, s * kk:],
                                             scan[:, cur, 0:(NB - s) * kk], ALU.add))
                cur, s = 1 - cur, 2 * s
            ranks = scan[:, cur, :]
            then(nc.vector.tensor_tensor(ranks, ranks, ps[7][:, :], ALU.subtract))
            then(nc.vector.tensor_tensor(ranks, ranks, ps[6][:, :], ALU.add))
            ch = chosen[:, :, :, :].rearrange("p b k e -> p (b k e)")
            then(nc.vector.tensor_scalar(ranks, ranks, float(CAPACITY), None, ALU.is_le))
            then(nc.vector.tensor_tensor(ranks, ranks, ch, ALU.mult))
            rk = ranks.rearrange("p (c e) -> p c e", e=NE)
            then(nc.vector.tensor_tensor(rk, rk, bcast(topw[:, :, :].rearrange("p b k -> p (b k)"), NE), ALU.mult))
            r4 = ranks.rearrange("p (b k e) -> p b k e", k=TOPK, e=NE)
            then(nc.vector.tensor_tensor(comb[:, :, :], r4[:, :, 0, :], r4[:, :, 1, :], ALU.add))
            then(nc.vector.tensor_scalar(comb[:, :, :], comb[:, :, :], 1.0 / (H_SCALE * W_SCALE), None, ALU.mult))
            dve.sem_inc(routed)

            def add_up(c, e, have_before):
                t = NE * c + e
                dve.wait_ge(f_y, t + 1)
                if have_before:
                    dve.wait_ge(f_acc, t)
                for r in range(CB):
                    n = CB * c + r
                    last = nc.vector.scalar_tensor_tensor(out=x_all[:, n, :], in0=ps[4 + e % 2][:, r * P:(r + 1) * P],
                                                          scalar=comb[:, n, e:e + 1], in1=x_all[:, n, :],
                                                          op0=ALU.mult, op1=ALU.add)
                last.then_inc(f_acc, 1)

            def experts(c, first):
                for e in range(NE):
                    t = NE * c + e
                    for i in range(HT):
                        dve.wait_ge(f_s, HT * t + i + 1)
                        if not (first and e == 0):
                            dve.wait_ge((f_lo0, f_lo1)[i], t)
                        nc.vector.scalar_tensor_tensor(out=hT[:, i, :], in0=ps[2 + i][:, :],
                                                       scalar=H_SCALE / (NORM_SCALE * W_SCALE), in1=silu[:, i, :],
                                                       op0=ALU.mult, op1=ALU.mult).then_inc(f_h, 1)
                    dve.wait_ge(f_hi, HT * t + HT)
                    nc.vector.tensor_tensor(h_lo[:, e % 2, 1, :], hT[:, 1, :], h_hi[:, e % 2, 1, :],
                                            ALU.subtract).then_inc(f_lo1, 1)
                    if e > 0:
                        add_up(c, e - 1, not (first and e == 1))
                    elif not first:
                        add_up(c - 1, NE - 1, True)

            experts(0, True)
            with dve.Fori(1, NC) as c:
                experts(c, False)
            add_up(NC - 1, NE - 1, True)

        @block.tensor
        def _(pe):
            def mm(o, l, r, start=True, stop=True, **kw):
                return nc.tensor.matmul(o, l, r, start=start, stop=stop, **kw)

            def self_attention(b, parity, valid, steps):
                for g in steps:
                    if g == 3 and valid(2):
                        pe.wait_ge(a_xn, b + 3)
                        if valid(-2):
                            pe.wait_ge(a_res, b - 1)
                        nc.tensor.transpose(ps[7][:, 0:P], xn[:, :], ident[:, :]).then_inc(a_xT, 1)
                    if g == 2 and valid(0) and not valid(-1):
                        pe.wait_ge(raw_ev, 3)
                        pe.wait_ge(rep_ready, 8)
                        pe.wait_ge(bo_ready, 1)
                    if valid(0):
                        t = G1 * b + g
                        if g == 0:
                            pe.wait_ge(a_evq, 4 * b + 4)
                        if g >= 2 or valid(-1):
                            pe.wait_ge(a_exp, t - 1)
                        bank = ps[g % 2]
                        mm(bank[:, :], ident_b[:, :], causal[:, :, :].rearrange("p h k -> p (h k)"), True, False)
                        for i in range(HPG):
                            h = HPG * g + i
                            last = mm(bank[:, i * P:(i + 1) * P], qz[:, parity, h // 2, h % 2, :],
                                      kT[:, parity, h // 2, :], False, i == HPG - 1)
                        last.then_inc(a_s, 1)
                    off, u, par = back(b, parity, g, 3, G1)
                    if valid(off):
                        t = G1 * (b + off) + u
                        pe.wait_ge(a_pTe, t + 1)
                        if u == 0:
                            pe.wait_ge(a_evv, 2 * (b + off) + 2)
                        if u > 0 or valid(off - 1):
                            pe.wait_ge(a_ze, t)
                        for i in range(HPG):
                            h = HPG * u + i
                            a = h % 2
                            last = mm(ps[6][64 * a:64 * a + 64, (i // 2) * P:(i // 2 + 1) * P],
                                      v1[:, par, h * E1:(h + 1) * E1], probsT[:, u % 2, i * P:(i + 1) * P])
                        last.then_inc(a_zz, 1)
                    off, u, par = back(b, parity, g, 2, G1)
                    if valid(off):
                        t = G1 * (b + off) + u
                        pe.wait_ge(a_norm, t + 1)
                        if u >= 2 or valid(off - 1):
                            pe.wait_ge(a_pTe, t - 1)
                        for i in range(HPG):
                            last = nc.tensor.transpose(ps[2 + u % 2][:, i * P:(i + 1) * P],
                                                       probs[:, u, i * P:(i + 1) * P], ident[:, :])
                        last.then_inc(a_pT, 1)
                    if g == 3 and valid(-1):
                        n = b - 1
                        pe.wait_ge(a_ze, G1 * n + G1)
                        if valid(2):
                            pe.wait_ge(a_xTe, b + 3)
                        if not valid(0):
                            pe.wait_ge(b_vve, 1)
                        for i in range(PAIRS):
                            last = mm(ps[7][:, P:2 * P], zT[:, i, :], wo[:, i, :], i == 0, i == PAIRS - 1)
                        last.then_inc(a_o, 1)
                    if valid(1) and g < 3:
                        n = b + 1
                        if not valid(0):
                            pe.wait_ge(w1_split, g + 1)
                        if g == 0:
                            pe.wait_ge(a_xlo, n + 1)
                        for half in range(2):
                            if g == 0 and valid(0):
                                pe.wait_ge(a_evv, 2 * n + half - 1)
                            if g > 0:
                                pe.wait_ge(a_evq, 4 * n + 2 * g + half - 1)
                            parts = ((w1_hi, xT_hi), (w1_hi, xT_lo), (w1_lo, xT_hi))
                            if g < 2:
                                for i in range(4):
                                    pair = 4 * half + i
                                    for k, (w, xs) in enumerate(parts):
                                        last = mm(ps[4 + half][:, i * P:(i + 1) * P],
                                                  w[:, g, 2 * pair:2 * pair + 2, :].rearrange("p h e -> p (h e)"),
                                                  xs[:, :], k == 0, k == 2)
                            else:
                                for k, (w, xs) in enumerate(parts):
                                    last = mm(ps[4 + half][:, :], xs[:, :],
                                              w[:, g, 8 * half:8 * half + 8, :].rearrange("p h e -> p (h e)"),
                                              k == 0, k == 2)
                            last.then_inc(a_fill, 1)

            def prepare():
                pe.wait_ge(ld_b, 48)
                pe.wait_ge(ln_ready, 1)
                for i in range(3):
                    last = nc.tensor.transpose(ps[1][:, PAIRS * i:PAIRS * (i + 1)], raw_b[:, i, :],
                                               ident[0:PAIRS, 0:PAIRS])
                last.then_inc(b1_T, 1)

            def prepare_cross():
                pe.wait_ge(ld_s, 16 * 3)
                for i in range(4):
                    last = nc.tensor.transpose(ps[3][:, i * P:(i + 1) * P], raw_s[:, i, :], ident[:, :])
                last.then_inc(raw_T, 1)
                nc.tensor.transpose(ps[6][:, P:P + NE], raw_s[0:NE, 4, :], ident[0:NE, 0:NE]).then_inc(raw_T, 1)
                pe.wait_ge(bv_spread, 1)
                pe.wait_ge(ld_wo, 32)
                for i in range(PAIRS):
                    last = mm(ps[6][:, 0:P], bv_wide[:, i * P:(i + 1) * P], wo[:, i, :], i == 0, i == PAIRS - 1)
                last.then_inc(bvo, 1)

            def wait_pT(row, u):
                of_vector = len([k for k in PT_ON_VECTOR if k <= u])
                if u in PT_ON_VECTOR:
                    pe.wait_ge(b_pTv, len(PT_ON_VECTOR) * row + of_vector)
                else:
                    pe.wait_ge(b_pTa, (G2 - len(PT_ON_VECTOR)) * row + u + 1 - of_vector)

            def cross_attention(b, parity, valid, steps):
                n = b + 1
                for g in steps:
                    if valid(0):
                        t = G2 * b + g
                        if g == 0:
                            pe.wait_ge(b_pack, 3 * b + 3)
                        before = [k for k in range(g) if SCORE_BANKS2[k] == SCORE_BANKS2[g]]
                        lag = g - before[-1] if before else g + G2 - max(k for k in range(G2) if SCORE_BANKS2[k] == SCORE_BANKS2[g])
                        if before or valid(-1):
                            pe.wait_ge(b_exp, t - lag + 1)
                        for i in range(2):
                            last = mm(ps[SCORE_BANKS2[g]][:, i * KEYS2:(i + 1) * KEYS2], qm[:, parity, 2 * g + i, :],
                                      kT2[:, parity, head2(2 * g + i) // 4, :])
                        last.then_inc(b_s, 1)
                    off, u, par = back(b, parity, g, 2, G2)
                    if valid(off):
                        t = G2 * (b + off) + u
                        pe.wait_ge(b_exp, t + 1)
                        if u >= 2 or valid(off - 1):
                            wait_pT(b + off - (u < 2), (u - 2) % G2)
                        for i in range(4):
                            last = nc.tensor.transpose(ps[2 + u % 2][:, i * P:(i + 1) * P],
                                                       probs[:, u % 4, i * P:(i + 1) * P], ident[:, :])
                        last.then_inc(b_pT, 1)
                    off, u, par = back(b, parity, g, 4, G2)
                    if valid(off):
                        wait_pT(b + off, u)
                        if u == 0:
                            pe.wait_ge(b_vc, b + off + 1)
                            pe.wait_ge(b_vve, b + off + 1)
                            if valid(off - 1):
                                pe.wait_ge(b_ze, b + off)
                        for k in range(2):
                            for i in range(2):
                                h = head2(2 * u + i)
                                q4, j = h // 4, h % 4
                                at = VPAD + VGAP * h - E2 * j
                                last = mm(ps[6][32 * q4:32 * q4 + 32, 0:P], vm[:, par, k, at:at + 32],
                                          probsT[:, u % 4, (2 * i + k) * P:(2 * i + k + 1) * P],
                                          j == 0 and k == 0, j == 3 and k == 1)
                        if u == G2 - 1:
                            last.then_inc(b_zz, 1)
                    if g == 0 and valid(1):
                        pe.wait_ge(b_xn, n + 1)
                        if valid(0):
                            pe.wait_ge(b_vve, b + 1)
                        else:
                            pe.wait_ge(a_res, NB - 2)
                        nc.tensor.transpose(ps[7][:, 0:P], xn2[:, :], ident[:, :]).then_inc(b_xT, 1)
                    if g == 1 and valid(-2):
                        pe.wait_ge(d_xn, b - 1)
                        if valid(1):
                            pe.wait_ge(b_xTe, n + 1)
                        nc.tensor.transpose(ps[7][:, 2 * P:3 * P], xn3[:, :], ident[:, :]).then_inc(d_xT, 1)
                    if g == 2 and valid(-1):
                        pe.wait_ge(b_wide, b)
                        if valid(1):
                            pe.wait_ge(b_xTe, n + 1)
                        if valid(-2):
                            pe.wait_ge(d_xTe, b - 1)
                        nc.tensor.transpose(ps[7][:, P:2 * P], rinv_wide[:, :, :].rearrange("p h e -> p (h e)"),
                                            ident[:, :]).then_inc(b_rT, 1)
                    if g == 2 and valid(-2):
                        pe.wait_ge(d_xTe, b - 1)
                        mm(ps[7][:, 3 * P:3 * P + NE], xT3[:, :], gateT[:, :]).then_inc(d_lg, 1)
                    if g == 4 and valid(-1):
                        pe.wait_ge(b_ze, b)
                        if valid(-2):
                            pe.wait_ge(d_lge, b - 1)
                        mm(ps[7][:, P:2 * P], zT2[:, :], wprojT[:, :]).then_inc(b_pr, 1)
                    if g == 0 and valid(1):
                        pe.wait_ge(b_keys4, n + 1)
                        if valid(0):
                            pe.wait_ge(b_pack, 3 * n)
                        else:
                            pe.wait_ge(a_evv, 2 * NB)
                        for q4 in range(4):
                            last = mm(ps[4][:, q4 * P:(q4 + 1) * P],
                                      keys4[:, q4, :, :, :].rearrange("p a l c -> p (a l c)"), ident_h[:, :])
                        last.then_inc(b_fill, 1)
                    if g in (2, 4) and valid(1):
                        pe.wait_ge(b_xTe, n + 1)
                        pe.wait_ge(b_pack, 3 * n + g // 2)
                        w = wqR if g == 2 else wkR
                        for q4 in range(4):
                            last = mm(ps[4][:, q4 * P:(q4 + 1) * P],
                                      w[:, q4, :, :].rearrange("p a c -> p (a c)"), xT2[:, :])
                        last.then_inc(b_fill, 1)
                    if g == 6 and valid(1):
                        if valid(-1):
                            pe.wait_ge(b_res, b)
                        else:
                            pe.wait_ge(a_res, NB - 1)
                        mm(ps[7][:, 0:P], xT2[:, :], wqkvT[:, 2, :]).then_inc(b_vv, 1)

            pe.wait_ge(c_sel, 9)
            pe.wait_ge(ld_ln, 32)
            nc.tensor.transpose(ps[1][:, 0:2], raw_ln[:, :], ident[0:2, 0:2]).then_inc(ln_T, 1)
            run_batches(pe, -2, NB - 2, self_attention, range(G1), {-2: prepare, -1: prepare_cross})
            run_joined(self_attention, cross_attention)
            pe.wait_ge(a_res, NB)
            pe.wait_ge(a_ze, G1 * NB)
            run_batches(pe, 0, NB + 2, cross_attention, range(G2))

            pe.wait_ge(ld_raw, 48)
            pe.wait_ge(d_lge, NB)

            def transpose_weights(e):
                if e == 2:
                    pe.wait_ge(routed, 1)
                if e > 2:
                    pe.wait_ge(w_staged, e)
                a, b = weight_banks(e)
                for i in range(HT):
                    nc.tensor.transpose(ps[a][:, i * P:(i + 1) * P], raw_gu[:, HT * e + i, :], ident[:, :])
                    nc.tensor.transpose(ps[a][:, (HT + i) * P:(HT + i + 1) * P], raw_gu[:, HT * (NE + e) + i, :],
                                        ident[:, :])
                for i in range(HT):
                    last = nc.tensor.transpose(ps[b][:, i * P:(i + 1) * P], raw_d[:, HT * e + i, :], ident[:, :])
                last.then_inc(w_T, 1)

            transpose_weights(0)
            transpose_weights(1)

            pe.wait_ge(r_chosen, 1)
            pe.wait_ge(d_cp, NB)
            mm(ps[6][:, :], upto[:, :], chosen_b[:, :]).then_inc(r_count_ps, 1)
            mm(ps[7][:, :], ones_b[:, :], chosen_b[:, :]).then_inc(r_count_ps, 1)

            def down(c, e, wait_bank):
                t = NE * c + e
                pe.wait_ge(f_hi, HT * t + HT)
                pe.wait_ge(f_lo0, t + 1)
                pe.wait_ge(f_lo1, t + 1)
                if wait_bank:
                    pe.wait_ge(f_acc, t - 1)
                for r in range(CB):
                    for i in range(HT):
                        own = slice(r * P, (r + 1) * P)
                        for k, (h, v) in enumerate(((h_hi, w_hi), (h_hi, w_lo), (h_lo, w_hi))):
                            last = mm(ps[4 + e % 2][:, own], h[:, e % 2, i, own], v[:, e, 2 * HT + i, :],
                                      i == 0 and k == 0, i == HT - 1 and k == 2)
                last.then_inc(f_y, 1)

            def experts(c, first):
                own = slice(0, CB) if first else bass.ds(CB * c, CB)
                rows_hi = xnT_hi[:, own, :].rearrange("p b t -> p (b t)")
                rows_lo = xnT_lo[:, own, :].rearrange("p b t -> p (b t)")
                for e in range(NE):
                    if first:
                        pe.wait_ge(w_ev, max(e + 1, 2))
                    for i in range(HT):
                        if not (first and e == 0):
                            pe.wait_ge(f_h, HT * NE * c + HT * e + i - 1)
                        for j in range(2):
                            w = HT * j + i
                            mm(ps[2 * j + i][:, :], w_hi[:, e, w, :], rows_hi, True, False)
                            mm(ps[2 * j + i][:, :], w_hi[:, e, w, :], rows_lo, False, False)
                            last = mm(ps[2 * j + i][:, :], w_lo[:, e, w, :], rows_hi, False, True)
                        last.then_inc(f_gu, 1)
                    if first and e + 2 < NE:
                        transpose_weights(e + 2)
                    if e > 0:
                        down(c, e - 1, not (first and e < 3))
                    elif not first:
                        down(c - 1, NE - 1, True)

            experts(0, True)
            with pe.Fori(1, NC) as c:
                experts(c, False)
            down(NC - 1, NE - 1, True)


_INS = ["x", "ctx_2048", "L0_attn_W_q", "L0_attn_W_k", "L0_attn_W_v", "L0_attn_W_o", "L0_attn_b_q", "L0_attn_b_k",
        "L0_attn_b_v", "L0_attn_b_o", "L0_attn_ln_w", "L0_attn_ln_b", "L0_xattn_w_qkv", "L0_xattn_w_proj",
        "L0_xattn_b_proj", "L0_ffn_gate_w", "L0_ffn_gate_proj_w", "L0_ffn_up_proj_w", "L0_ffn_down_proj_w"]


def kernel(**inputs):
    import numpy as np
    from concourse import bacc
    from concourse.bass_utils import run_bass_kernel_spmd

    nc = bacc.Bacc("TRN2", target_bir_lowering=False, num_devices=1)
    arrays, args = {}, []
    for name in _INS:
        a = np.ascontiguousarray(inputs[name])
        arrays[f"in_{name}"] = a
        args.append(nc.dram_tensor(f"in_{name}", a.shape, mybir.dt.from_np(a.dtype), kind="ExternalInput").ap())
    args.append(nc.dram_tensor("out_x", (NB, P, D), F32, kind="ExternalOutput").ap())
    build(nc, *args)
    return run_bass_kernel_spmd(nc, [arrays], core_ids=[0]).results[0]["out_x"]
```
